# Optimizing a Trainium2 kernel written in Bass

```python
import numpy as np
import jax
import jax.numpy as jnp

def _softmax(x, axis=-1):
    return jax.nn.softmax(x, axis=axis)

def _gelu(x):
    return jax.nn.gelu(x, approximate=True)

def _silu(x):
    return jax.nn.silu(x)

def _sigmoid(x):
    return jax.nn.sigmoid(x)

def _layernorm(x, axis=-1, eps=1e-05):
    m = jnp.mean(x, axis=axis, keepdims=True)
    v = jnp.var(x, axis=axis, keepdims=True)
    return (x - m) / jnp.sqrt(v + eps)

def _scatter_add(tgt, idx, src, axis=0):
    return tgt.at[idx].add(src)

def _segment_sum(src, seg, n):
    return jax.ops.segment_sum(src, seg, n)
kernel_name = 'mk_cond_seq_d1_seqx_r4_0988b1'

def setup_inputs(seed: int=0):
    np.random.seed(seed)
    _w = jnp.asarray

    def _rec_inputs():
        import jax
        import jax.numpy as jnp
        _rk = jax.random.key(seed)
        x = -0.0002928 + 1 * jax.random.normal(jax.random.fold_in(_rk, 1), (8, 512, 256), jnp.float32)
        _lenS = 512 - jax.random.randint(jax.random.fold_in(_rk, 7), (8,), 0, max(1, 512 // 4) + 1, jnp.int32)
        _lenS2 = 512 - jax.random.randint(jax.random.fold_in(_rk, 8), (8,), 0, max(1, 512 // 4) + 1, jnp.int32)
        itok_B_6_14 = jax.random.randint(jax.random.fold_in(_rk, 11), (8,), 6, 15, jnp.int32)
        return (x, itok_B_6_14)
    x, itok_B_6_14 = _rec_inputs()

    def _L0_cond_setup():
        import jax, jax.numpy as jnp
        import numpy as np
        D = 256
        E = 8
        FF = 1024
        TOPK = 2
        S = 32
        SE = 64
        SH = 128
        B, T = (2, 512)

        def _forward(x, subject_ids, ln_g, ln_b, subj_emb, hyp_w1, hyp_b1, hyp_w2, hyp_b2, sty_w1, sty_b1, sty_w2, sty_b2, router_w, exp_w1, exp_b1, exp_w2, exp_b2):
            mu = x.mean(-1, keepdims=True)
            var = x.var(-1, keepdims=True)
            h = (x - mu) * jax.lax.rsqrt(var + 1e-05) * ln_g + ln_b
            m_t = h.mean(1, keepdims=True)
            v_t = h.var(1, keepdims=True)
            h_norm = (h - m_t) * jax.lax.rsqrt(v_t + 1e-08)
            se = subj_emb[subject_ids]
            hyp = jax.nn.relu(se @ hyp_w1 + hyp_b1) @ hyp_w2 + hyp_b2
            sty = jax.nn.relu(hyp @ sty_w1 + sty_b1) @ sty_w2 + sty_b2
            gamma, beta = jnp.split(sty, 2, axis=-1)
            gamma = jax.nn.softplus(gamma) + 1e-08
            h = h_norm * gamma[:, None, :] + beta[:, None, :]
            h_flat = h.reshape(-1, D)
            probs = jax.nn.softmax(h_flat @ router_w, axis=-1)
            gates, idx = jax.lax.top_k(probs, TOPK)
            gates = gates / gates.sum(-1, keepdims=True)
            N = h_flat.shape[0]
            combine = jnp.zeros((N, E), h_flat.dtype).at[jnp.arange(N)[:, None], idx].add(gates)
            hid = jax.nn.relu(jnp.einsum('nd,edf->nef', h_flat, exp_w1) + exp_b1)
            eout = jnp.einsum('nef,efd->ned', hid, exp_w2) + exp_b2
            y = jnp.einsum('ned,ne->nd', eout, combine)
            return x + y.reshape(x.shape)
        key = jax.random.key(seed)
        ks = jax.random.split(key, 16)
        n = lambda k, sh, s=0.02: jax.random.normal(k, sh, dtype=jnp.float32) * s
        return {'x': jax.random.normal(ks[0], (B, T, D), dtype=jnp.float32), 'subject_ids': jax.random.randint(ks[1], (B,), 0, S), 'ln_g': jnp.ones((D,), jnp.float32), 'ln_b': jnp.zeros((D,), jnp.float32), 'subj_emb': n(ks[2], (S, SE)), 'hyp_w1': n(ks[3], (SE, SH), 1.0 / np.sqrt(SE)), 'hyp_b1': jnp.zeros((SH,), jnp.float32), 'hyp_w2': n(ks[4], (SH, SH), 1.0 / np.sqrt(SH)), 'hyp_b2': jnp.zeros((SH,), jnp.float32), 'sty_w1': n(ks[5], (SH, SH // 2), 1.0 / np.sqrt(SH)), 'sty_b1': jnp.zeros((SH // 2,), jnp.float32), 'sty_w2': n(ks[6], (SH // 2, 2 * D), 1.0 / np.sqrt(SH // 2)), 'sty_b2': jnp.zeros((2 * D,), jnp.float32), 'router_w': n(ks[7], (D, E), 1.0 / np.sqrt(D)), 'exp_w1': n(ks[8], (E, D, FF), 1.0 / np.sqrt(D)), 'exp_b1': jnp.zeros((E, FF), jnp.float32), 'exp_w2': n(ks[9], (E, FF, D), 1.0 / np.sqrt(FF)), 'exp_b2': jnp.zeros((E, D), jnp.float32)}
    _L0_cond_all = _L0_cond_setup()
    _L0_cond_in = {k: v for k, v in _L0_cond_all.items() if k in ('ln_g', 'ln_b', 'subj_emb', 'hyp_w1', 'hyp_b1', 'hyp_w2', 'hyp_b2', 'sty_w1', 'sty_b1', 'sty_w2', 'sty_b2', 'router_w', 'exp_w1', 'exp_b1', 'exp_w2', 'exp_b2')}
    del _L0_cond_all
    return {'x': x, 'itok_B_6_14': itok_B_6_14, 'L0_cond_ln_g': _L0_cond_in['ln_g'], 'L0_cond_ln_b': _L0_cond_in['ln_b'], 'L0_cond_subj_emb': _L0_cond_in['subj_emb'], 'L0_cond_hyp_w1': _L0_cond_in['hyp_w1'], 'L0_cond_hyp_b1': _L0_cond_in['hyp_b1'], 'L0_cond_hyp_w2': _L0_cond_in['hyp_w2'], 'L0_cond_hyp_b2': _L0_cond_in['hyp_b2'], 'L0_cond_sty_w1': _L0_cond_in['sty_w1'], 'L0_cond_sty_b1': _L0_cond_in['sty_b1'], 'L0_cond_sty_w2': _L0_cond_in['sty_w2'], 'L0_cond_sty_b2': _L0_cond_in['sty_b2'], 'L0_cond_router_w': _L0_cond_in['router_w'], 'L0_cond_exp_w1': _L0_cond_in['exp_w1'], 'L0_cond_exp_b1': _L0_cond_in['exp_b1'], 'L0_cond_exp_w2': _L0_cond_in['exp_w2'], 'L0_cond_exp_b2': _L0_cond_in['exp_b2']}

def reference(x, itok_B_6_14, L0_cond_ln_g, L0_cond_ln_b, L0_cond_subj_emb, L0_cond_hyp_w1, L0_cond_hyp_b1, L0_cond_hyp_w2, L0_cond_hyp_b2, L0_cond_sty_w1, L0_cond_sty_b1, L0_cond_sty_w2, L0_cond_sty_b2, L0_cond_router_w, L0_cond_exp_w1, L0_cond_exp_b1, L0_cond_exp_w2, L0_cond_exp_b2):
    import jax
    import jax.numpy as jnp

    def _L0_cond_ref(x, subject_ids, ln_g, ln_b, subj_emb, hyp_w1, hyp_b1, hyp_w2, hyp_b2, sty_w1, sty_b1, sty_w2, sty_b2, router_w, exp_w1, exp_b1, exp_w2, exp_b2):
        import jax, jax.numpy as jnp
        import numpy as np
        D = 256
        E = 8
        FF = 1024
        TOPK = 2
        S = 32
        SE = 64
        SH = 128
        B, T = (2, 512)

        def _forward(x, subject_ids, ln_g, ln_b, subj_emb, hyp_w1, hyp_b1, hyp_w2, hyp_b2, sty_w1, sty_b1, sty_w2, sty_b2, router_w, exp_w1, exp_b1, exp_w2, exp_b2):
            mu = x.mean(-1, keepdims=True)
            var = x.var(-1, keepdims=True)
            h = (x - mu) * jax.lax.rsqrt(var + 1e-05) * ln_g + ln_b
            m_t = h.mean(1, keepdims=True)
            v_t = h.var(1, keepdims=True)
            h_norm = (h - m_t) * jax.lax.rsqrt(v_t + 1e-08)
            se = subj_emb[subject_ids]
            hyp = jax.nn.relu(se @ hyp_w1 + hyp_b1) @ hyp_w2 + hyp_b2
            sty = jax.nn.relu(hyp @ sty_w1 + sty_b1) @ sty_w2 + sty_b2
            gamma, beta = jnp.split(sty, 2, axis=-1)
            gamma = jax.nn.softplus(gamma) + 1e-08
            h = h_norm * gamma[:, None, :] + beta[:, None, :]
            h_flat = h.reshape(-1, D)
            probs = jax.nn.softmax(h_flat @ router_w, axis=-1)
            gates, idx = jax.lax.top_k(probs, TOPK)
            gates = gates / gates.sum(-1, keepdims=True)
            N = h_flat.shape[0]
            combine = jnp.zeros((N, E), h_flat.dtype).at[jnp.arange(N)[:, None], idx].add(gates)
            hid = jax.nn.relu(jnp.einsum('nd,edf->nef', h_flat, exp_w1) + exp_b1)
            eout = jnp.einsum('nef,efd->ned', hid, exp_w2) + exp_b2
            y = jnp.einsum('ned,ne->nd', eout, combine)
            return x + y.reshape(x.shape)
        return _forward(x, subject_ids, ln_g, ln_b, subj_emb, hyp_w1, hyp_b1, hyp_w2, hyp_b2, sty_w1, sty_b1, sty_w2, sty_b2, router_w, exp_w1, exp_b1, exp_w2, exp_b2)
    x = _L0_cond_ref(x, itok_B_6_14, L0_cond_ln_g, L0_cond_ln_b, L0_cond_subj_emb, L0_cond_hyp_w1, L0_cond_hyp_b1, L0_cond_hyp_w2, L0_cond_hyp_b2, L0_cond_sty_w1, L0_cond_sty_b1, L0_cond_sty_w2, L0_cond_sty_b2, L0_cond_router_w, L0_cond_exp_w1, L0_cond_exp_b1, L0_cond_exp_w2, L0_cond_exp_b2)
    return x

_drawn_inputs = setup_inputs


def setup_inputs(seed=0):
    import zlib

    import numpy as np

    out = dict(_drawn_inputs(seed))
    spreads = {'L0_cond_ln_g': (1.0, 0.2),
     'L0_cond_ln_b': (0.0, 0.1),
     'L0_cond_hyp_b1': (0.0, 0.1),
     'L0_cond_hyp_b2': (0.0, 0.1),
     'L0_cond_sty_b1': (0.0, 0.1),
     'L0_cond_sty_b2': (0.0, 0.1),
     'L0_cond_exp_b1': (0.0, 0.1),
     'L0_cond_exp_b2': (0.0, 0.1)}
    factors = {}
    for name, (base, spread) in spreads.items():
        noise = np.random.default_rng([zlib.crc32(name.encode()), seed]).standard_normal(out[name].shape)
        drawn = base * np.exp(spread * noise) if base else spread * noise
        out[name] = jnp.asarray(drawn.astype(out[name].dtype))
    for name, factor in factors.items():
        out[name] = (out[name] * factor).astype(out[name].dtype)
    return out
```

```python
from contextlib import ExitStack

import concourse.bass as bass
from concourse import mybir

F32 = mybir.dt.float32
F16 = mybir.dt.float16
I32 = mybir.dt.int32
ALU = mybir.AluOpType
ACT = mybir.ActivationFunctionType
AX_X = mybir.AxisListType.X

P = 128
B, T, D = 8, 512, 256
E, FF = 8, 1024
NSUBJ, SE, SH = 32, 64, 128
N = B * T
KD = D // P
FC = FF // P
JB = T // P
NJ = N // P
NBLK = E * NJ
NH = NBLK // P
TILES = (2 * N + E * (P - 1)) // P
ROWS = N + P + 8
WSCALE = 64.0
LN_EPS, T_EPS = 1e-5, 1e-8
UNIT = 2 * FF
UNITS = 2 * E
NSTAGE = 3
VEC_ROWS = 75
V_LNG, V_LNB, V_HB1, V_HB2, V_SB1, V_SB2 = 64, 66, 68, 69, 70, 71

C_ID, C_SLOT, C_NEGT, C_SLOTCOL, C_Q, C_DJ, C_DESC, C_TOK2, C_T128 = 0, 128, 256, 328, 400, 401, 405, 413, 415
C_END = C_T128 + 72


def moe_kernel(nc, x, ids, ln_g, ln_b, subj_emb, hyp_w1, hyp_b1, hyp_w2, hyp_b2, sty_w1, sty_b1,
               sty_w2, sty_b2, router_w, exp_w1, exp_b1, exp_w2, exp_b2, consts, consts16, out):
    h_dram = nc.dram_tensor("h_rows", (ROWS, D), F32).ap()
    comb_dram = nc.dram_tensor("comb_rows", (ROWS, E), F32).ap()
    x_v = x.rearrange("b (p j) d -> b p (j d)", j=JB)
    out_v = out[0:N, :].rearrange("(b p j) d -> b p (j d)", b=B, j=JB)
    h_v = h_dram[0:N, :].rearrange("(b p j) d -> b p (j d)", b=B, j=JB)
    comb_v = comb_dram[0:N, :].rearrange("(b p j) e -> p b (j e)", b=B, j=JB)
    w1_v = exp_w1.rearrange("e (k p) f -> e p k f", p=P)
    w2_v = exp_w2.rearrange("e (c p) d -> e p c d", p=P)

    def w_v(u):
        return (w2_v if u % 2 else w1_v)[u // 2]

    with ExitStack() as ctx:
        def sb(name, shape, dt=F32):
            return ctx.enter_context(nc.sbuf_tensor(name, shape, dt))

        def sem(name):
            return ctx.enter_context(nc.semaphore(name))

        whi = sb("whi", [P, UNITS * UNIT], F16)
        wlo = sb("wlo", [P, UNITS * UNIT], F16)
        stage = sb("stage", [P, NSTAGE, UNIT])
        b2row = stage[:, 1, :]
        cst = sb("cst", [P, C_END])
        c16 = sb("c16", [P, 2 * P], F16)

        xs = sb("xs", [P, 2, JB * D])
        xn = sb("xn", [P, 2, JB * D])
        hT = sb("hT", [P, 2, KD * T])
        h2T = sb("h2T", [P, 2, KD * T])
        hrow = sb("hrow", [P, 2, JB * D])
        hid32 = hT[:, 0, :]
        hidhi = h2T[:, 0, :].bitcast(F16).rearrange("p (a f) -> p a f", a=2)
        hidlo = h2T[:, 1, :].bitcast(F16).rearrange("p (a f) -> p a f", a=2)
        hg = xs[:, 0, 0:2 * D].rearrange("p (a d) -> p a d", a=2)
        ysum = xs[:, 0, 2 * D:4 * D].rearrange("p (a d) -> p a d", a=2)
        yout = xs[:, 1, 0:2 * D].rearrange("p (a d) -> p a d", a=2)
        hThi = xn[:, 0, 0:D].bitcast(F16).rearrange("p (a d) -> p a d", a=2)
        hTlo = xn[:, 0, D:2 * D].bitcast(F16).rearrange("p (a d) -> p a d", a=2)
        step16 = xn[:, 1, 0:2 * P].bitcast(F16).rearrange("p (a h s) -> p a h s", a=2, h=NH)
        junk = xn[:, 1, 2 * P:3 * P]

        hw1 = hrow[0:SE, 1, 0:SH]
        hw2 = hrow[:, 1, SH:2 * SH]
        sw1 = hrow[:, 1, 2 * SH:2 * SH + SH // 2]
        sw2 = hrow[0:SH // 2, 1, 320:320 + 2 * D]
        d1, d2, ex, oh1 = (hT[:, 1, i * NBLK:(i + 1) * NBLK] for i in range(4))
        tm = xn[:, 1, 3 * P:5 * P]
        csum, dstart = xn[:, 0, 2 * D:3 * D], xn[:, 0, 3 * D:4 * D]
        ones = xs[:, 1, 2 * D:3 * D]
        ge = hrow[:, 0, 0:72 * (E + 1)]

        vrows = sb("vrows", [P, P])
        vcol = sb("vcol", [P, VEC_ROWS])
        rw = sb("rw", [P, KD * E])
        idcol = sb("idcol", [B, 1], I32)
        se = sb("se", [B, SE])
        sT = sb("sT", [P, 4, B])
        gam = sb("gam", [P, KD * B])
        bet = sb("bet", [P, KD * B])
        sp = sb("sp", [P, 6, KD * B])
        bns = sb("bns", [P, JB, 6])
        mv = sb("mv", [P, 2, JB, 2])
        lnv = sb("lnv", [P, 2, 4, JB])
        tns = sb("tns", [P, KD, 6])
        tmv = sb("tmv", [P, 2, KD, 2])
        tnv = sb("tnv", [P, 2, 6, KD])
        lg = sb("lg", [P, NJ * E])
        selh = sb("selh", [P, NBLK + 1], F16)
        dsel = sb("dsel", [P, NBLK], F16)
        m8 = sb("m8", [P, 8, NJ])
        start = sb("start", [P, NBLK + 1])
        ne = sb("ne", [P, 6, E])
        nei = sb("nei", [P, 2, E], I32)
        stcol = sb("stcol", [P, 2 * NH])
        table = sb("table", [P, NH, P + 2], F16)
        ohe = sb("ohe", [P, 72 * E])
        etile = sb("etile", [P, 72], I32)
        tok = sb("tok", [P, 72], I32)
        gates = sb("gates", [P, 72])
        cg = sb("cg", [P, 2, E])
        gprod = sb("gprod", [P, 2, E])
        rt = sb("rt", [P, 2, 4])
        rj = sb("rj", [P, 2])
        idxg = [sb(f"idxg{i}", [P, 1], I32) for i in range(2)]
        idxs = [sb(f"idxs{i}", [P, 1], I32) for i in range(2)]
        zero = sb("zero", [P, D])
        held_gp = sb("held_gp", [1, 2])
        held_ve = sb("held_ve", [1, 1])

        banks = [ctx.enter_context(nc.psum_tensor(f"bank{i}", [P, 512], F32)) for i in range(8)]
        bk_T = banks[0:2]
        bk_back = banks[2:4]
        bk_log = banks[4:6]
        bk_small = banks[6]
        bk_cnt = banks[7]
        bk_hid = banks[0:2]
        bk_y = banks[2:4]
        bk_g = banks[4]
        bk_tab = banks[5]

        ident = cst[:, C_ID:C_ID + P]
        slotrow = cst[:, C_SLOT:C_SLOT + P]
        desc = cst[:, C_DESC:C_DESC + E]
        qcol = cst[:, C_Q:C_Q + 1]
        upto = c16[:, 0:P]
        ones16 = c16[:, P:2 * P]

        s_cst, s_ids, s_se = sem("constants_loaded"), sem("ids_loaded"), sem("subjects_gathered")
        s_par = sem("parameters_loaded")
        s_x = [sem(f"x_loaded{i}") for i in range(2)]
        s_w = [sem(f"weights_staged{i}") for i in range(NSTAGE)]
        s_b2 = sem("b2_loaded")
        s_init = sem("out_initialised")
        s_zero = sem("zeros_ready")
        s_spare = sem("spare_rows_written")
        s_vz = sem("vector_rows_cleared")
        s_small_pe, s_small_v, s_small_a = sem("style_products"), sem("style_vector_steps"), sem("style_scalar_steps")
        s_lnv, s_sd = sem("token_stats"), sem("token_deviation")
        s_nrm = sem("token_norm_ready")
        s_xn = sem("x_normalised")
        s_tr = sem("x_transposed")
        s_hT = sem("h_affine_done")
        s_tst, s_tsd, s_h2 = sem("time_stats"), sem("time_deviation"), sem("h_modulated")
        s_back, s_log = sem("h_rows_transposed"), sem("logits_done")
        s_hrow, s_hst = sem("h_rows_copied"), [sem(f"h_rows_stored{i}") for i in range(2)]
        s_lgc = sem("logits_copied")
        s_v = sem("vector_chain")
        s_d, s_exp = sem("logits_less_max"), sem("router_exp")
        s_sel, s_cnt, s_ds, s_dp = sem("selection_ready"), sem("counts_done"), sem("selection_steps_ready"), sem("prefix_done")
        s_comb, s_combst = sem("combine_ready"), sem("combine_stored")
        s_whi, s_wlo = sem("w_hi_ready"), [sem(f"w_lo_ready{i}") for i in range(NSTAGE)]
        s_et = sem("tile_experts_ready")
        s_step, s_tab, s_tok = sem("slot_steps_ready"), sem("slot_table_done"), sem("slot_tokens_ready")
        s_gh, s_gc = [sem(f"h_gathered{i}") for i in range(2)], [sem(f"combine_gathered{i}") for i in range(2)]
        s_gt, s_hi, s_lo = sem("tile_transposed"), sem("tile_hi_ready"), sem("tile_lo_ready")
        s_hm, s_relu, s_split = sem("hidden_products"), sem("hidden_relu"), sem("hidden_split")
        s_ym, s_ys, s_yo = sem("y_products"), sem("y_biased"), sem("y_gated")
        s_gate, s_idx, s_sc = sem("gates_ready"), sem("scatter_index_ready"), sem("y_scattered")
        s_held = [sem("gather_waits_carried"), sem("scatter_waits_carried")]
        s_dv, s_fin = sem("vector_tile_chain"), sem("finished")

        block = ctx.enter_context(nc.Block())

        @block.sync
        def _(sp_):
            sp_.dma_start(idcol[:, :], ids.rearrange("(b a) -> b a", a=1)).then_inc(s_ids, 16)
            sp_.dma_start(cst[:, :], consts).then_inc(s_cst, 16)
            sp_.dma_start(c16[:, :], consts16).then_inc(s_cst, 16)

            def load_x(b, par):
                if not (isinstance(b, int) and b < 2):
                    sp_.wait_ge(s_xn, b - 1)
                sp_.dma_start(xs[:, par, :], x_v[bass.ds(b, 1)].rearrange("b p n -> (b p) n")).then_inc(s_x[par], 16)

            load_x(0, 0)
            load_x(1, 1)
            sp_.wait_ge(s_vz, 1)
            sp_.dma_start(vrows[0:64, :], exp_b1.rearrange("e (c p) -> (e c) p", p=P)).then_inc(s_par, 16)
            for at, v in ((V_LNG, ln_g), (V_LNB, ln_b), (V_HB1, hyp_b1), (V_HB2, hyp_b2), (V_SB2, sty_b2)):
                sp_.dma_start(vrows[at:at + v.shape[0] // P, :], v.rearrange("(r p) -> r p", p=P)).then_inc(s_par, 16)
            sp_.dma_start(vrows[V_SB1:V_SB1 + 1, 0:SH // 2], sty_b1.rearrange("(r p) -> r p", r=1)).then_inc(s_par, 16)
            sp_.dma_start(hw1[:, :], hyp_w1).then_inc(s_par, 16)
            sp_.dma_start(hw2[:, :], hyp_w2).then_inc(s_par, 16)
            sp_.dma_start(sw1[:, :], sty_w1).then_inc(s_par, 16)
            sp_.dma_start(sw2[:, :], sty_w2).then_inc(s_par, 16)
            sp_.dma_start(rw[:, :].rearrange("p (k e) -> p k e", k=KD), router_w.rearrange("(k p) e -> p k e", p=P)).then_inc(s_par, 16)
            def load_weights(g, slot):
                if not (isinstance(g, int) and g == 0):
                    sp_.wait_ge(s_wlo[slot], g)
                src = w_v(NSTAGE * g + slot)
                sp_.dma_start(stage[:, slot, :].rearrange("p (a n) -> p a n", a=src.shape[1]), src).then_inc(s_w[slot], 16)

            for slot in range(NSTAGE):
                load_weights(0, slot)
            for g in range(1, B // 2):
                for par in range(2):
                    load_x(2 * g + par, par)
                for slot in range(NSTAGE):
                    load_weights(g, slot)
            for u in range(NSTAGE * (B // 2), UNITS):
                load_weights(u // NSTAGE, u % NSTAGE)
            sp_.dma_start(out[0:N, :], x.rearrange("b t d -> (b t) d")).then_inc(s_init, 16)
            sp_.wait_ge(s_wlo[1], len(range(1, UNITS, NSTAGE)))
            sp_.dma_start(b2row[:, :], exp_b2.rearrange("e d -> (e d)").partition_broadcast(P)).then_inc(s_b2, 16)
            sp_.wait_ge(s_init, 16)

        @block.gpsimd
        def _(gp):
            gp.memset(vrows[:, :], 0.0).then_inc(s_vz, 1)
            gp.memset(zero[:, :], 0.0).then_inc(s_zero, 1)
            gp.wait_ge(s_ids, 16)
            gp.indirect_dma_start(out=se[:, :], out_offset=None, in_=subj_emb,
                                  in_offset=bass.IndirectOffsetOnAxis(ap=idcol[:, 0:1], axis=0)).then_inc(s_se, 16)
            gp.wait_ge(s_zero, 1)
            gp.dma_start(h_dram[N:N + P, :], zero[:, :]).then_inc(s_spare, 16)
            gp.dma_start(h_dram[N + P:ROWS, :], zero[0:8, :]).then_inc(s_spare, 16)
            gp.dma_start(out[N:N + P, :], zero[:, :]).then_inc(s_spare, 16)
            gp.dma_start(out[N + P:ROWS, :], zero[0:8, :]).then_inc(s_spare, 16)
            gp.dma_start(comb_dram[N:N + P, :], zero[:, 0:E]).then_inc(s_spare, 16)
            gp.dma_start(comb_dram[N + P:ROWS, :], zero[0:8, 0:E]).then_inc(s_spare, 16)

            def carry(t, kind):
                if not (isinstance(t, int) and t == 0):
                    gp.wait_ge(s_held[kind], t)
                gp.tensor_tensor(held_gp[:, kind:kind + 1], zero[0:1, 0:1], zero[0:1, 0:1], ALU.add).then_inc(s_held[kind], 1)

            def gather(t, par):
                gp.wait_ge(s_tok, t + 1)
                if not (isinstance(t, int) and t < 2):
                    gp.wait_ge(s_gt, t - 1)
                    gp.wait_ge(s_gate, t - 1)
                carry(t, 0)
                gp.indirect_dma_start(out=hg[:, par, :], out_offset=None, in_=h_dram,
                                      in_offset=bass.IndirectOffsetOnAxis(ap=idxg[par][:, 0:1], axis=0)).then_inc(s_gh[par], 16)
                gp.indirect_dma_start(out=cg[:, par, :], out_offset=None, in_=comb_dram,
                                      in_offset=bass.IndirectOffsetOnAxis(ap=idxg[par][:, 0:1], axis=0)).then_inc(s_gc[par], 16)

            def scatter(t, par):
                if not (isinstance(t, int) and t == 0):
                    gp.wait_ge(s_sc, t * 16)
                gp.tensor_copy(idxs[par][:, :], tok[:, bass.ds(t, 1)]).then_inc(s_idx, 1)
                gp.wait_ge(s_idx, t + 1)
                gp.wait_ge(s_yo, t + 1)
                carry(t, 1)
                gp.indirect_dma_start(out=out, out_offset=bass.IndirectOffsetOnAxis(ap=idxs[par][:, 0:1], axis=0),
                                      in_=yout[:, par, :], in_offset=None, compute_op=ALU.add).then_inc(s_sc, 16)

            gp.wait_ge(s_hst[0], 16 * (B // 2))
            gp.wait_ge(s_hst[1], 16 * (B // 2))
            gp.wait_ge(s_spare, 16 * 6)
            gp.wait_ge(s_combst, 16)
            gp.wait_ge(s_init, 16)
            for t in range(3):
                gather(t, t % 2)
            gather(3, 1)
            gather(4, 0)
            scatter(0, 0)
            with gp.Fori(2, TILES - 3, 2) as i:
                for par in range(2):
                    gather(i + par + 3, 1 - par)
                    scatter(i + par - 1, 1 - par)
            for t in range(TILES - 3, TILES + 1):
                scatter(t - 1, (t - 1) % 2)
            gp.wait_ge(s_sc, 16 * TILES)

        @block.scalar
        def _(act):
            def style_softplus():
                act.wait_ge(s_small_v, 10)
                nc.scalar.activation(sp[:, 2, :], sp[:, 1, :], ACT.Exp).then_inc(s_small_a, 1)
                act.wait_ge(s_small_v, 11)
                nc.scalar.activation(sp[:, 4, :], sp[:, 3, :], ACT.Ln).then_inc(s_small_a, 1)

            def deviation(b, par):
                act.wait_ge(s_lnv, b + 1)
                nc.scalar.activation(lnv[:, par, 1, :], lnv[:, par, 0, :], ACT.Sqrt).then_inc(s_sd, 1)

            def normalise(b, par):
                act.wait_ge(s_nrm, b + 1)
                if not (isinstance(b, int) and b < 2):
                    act.wait_ge(s_tr, b - 1)
                for j in range(JB):
                    ins = nc.scalar.activation(xn[:, par, j * D:(j + 1) * D], xs[:, par, j * D:(j + 1) * D], ACT.Identity,
                                               bias=lnv[:, par, 3, j:j + 1], scale=lnv[:, par, 2, j:j + 1])
                ins.then_inc(s_xn, 1)

            def affine(b, par):
                act.wait_ge(s_tr, b + 1)
                if not (isinstance(b, int) and b < 2):
                    act.wait_ge(s_h2, b - 1)
                for k in range(KD):
                    ins = nc.scalar.activation(hT[:, par, k * T:(k + 1) * T], bk_T[k][:, :], ACT.Identity,
                                               bias=vcol[:, V_LNB + k:V_LNB + k + 1], scale=vcol[:, V_LNG + k:V_LNG + k + 1])
                ins.then_inc(s_hT, 1)

            def time_deviation(b, par):
                act.wait_ge(s_tst, b + 1)
                nc.scalar.activation(tnv[:, par, 1, :], tnv[:, par, 0, :], ACT.Sqrt).then_inc(s_tsd, 1)

            def rows(b, par):
                act.wait_ge(s_back, b + 1)
                if not (isinstance(b, int) and b < 2):
                    act.wait_ge(s_hst[par], (b - par) * 8)
                for g in range(2):
                    ins = nc.scalar.activation(hrow[:, par, g * 512:(g + 1) * 512], bk_back[g][:, :], ACT.Copy)
                ins.then_inc(s_hrow, 1)
                act.wait_ge(s_hrow, b + 1)
                act.dma_start(h_v[bass.ds(b, 1)].rearrange("b p n -> (b p) n"), hrow[:, par, :]).then_inc(s_hst[par], 16)

            def w_hi(g, slot):
                act.wait_ge(s_w[slot], 16 * g + 16)
                nc.scalar.activation(whi[:, bass.ds(g * (NSTAGE * UNIT) + slot * UNIT, UNIT)], stage[:, slot, :],
                                     ACT.Copy, scale=WSCALE).then_inc(s_whi, 1)

            act.wait_ge(s_small_v, 1)
            deviation(0, 0)
            normalise(0, 0)
            deviation(1, 1)
            affine(0, 0)
            normalise(1, 1)
            time_deviation(0, 0)
            style_softplus()
            with act.Fori(1, B // 2) as g:
                for par in range(2):
                    b = g * 2 + par
                    deviation(b, par)
                    affine(b - 1, 1 - par)
                    normalise(b, par)
                    time_deviation(b - 1, 1 - par)
                    w_hi(g - 1, par)
                    rows(b - 2, par)
                w_hi(g - 1, 2)
            affine(B - 1, 1)
            time_deviation(B - 1, 1)
            rows(B - 2, 0)
            rows(B - 1, 1)
            act.wait_ge(s_d, 1)
            nc.scalar.activation(ex[:, :], d1[:, :], ACT.Exp).then_inc(s_exp, 1)
            w_hi(B // 2 - 1, 0)
            w_hi(B // 2 - 1, 1)
            act.wait_ge(s_comb, 1)
            act.dma_start(comb_v, oh1[:, :].rearrange("p (b n) -> p b n", b=B)).then_inc(s_combst, 16)
            for u in range(NSTAGE * (B // 2 - 1) + 2, UNITS):
                w_hi(u // NSTAGE, u % NSTAGE)

            def relu(t, half, b1_t):
                act.wait_ge(s_hm, 2 * t + half + 1)
                if not (isinstance(t, int) and t == 0):
                    act.wait_ge(s_split, 2 * t + half - 1)
                for c in range(4 * half, 4 * half + 4):
                    ins = nc.scalar.activation(hid32[:, c * P:(c + 1) * P], bk_hid[half][:, (c - 4 * half) * P:(c - 4 * half + 1) * P],
                                               ACT.Relu, bias=vcol[:, bass.ds(b1_t * FC + c, 1)], scale=1.0 / WSCALE)
                ins.then_inc(s_relu, 1)

            def tile_hi(t, par):
                act.wait_ge(s_gt, t + 1)
                if not (isinstance(t, int) and t < 2):
                    act.wait_ge(s_hm, 2 * t - 2)
                nc.scalar.activation(hThi[:, par, :], bk_g[:, 0:D], ACT.Copy).then_inc(s_hi, 1)

            def gate_y(t, par):
                act.wait_ge(s_ys, t + 1)
                act.wait_ge(s_gate, t + 1)
                if not (isinstance(t, int) and t < 2):
                    act.wait_ge(s_sc, t * 16 - 16)
                nc.scalar.activation(yout[:, par, :], ysum[:, par, :], ACT.Copy, scale=gates[:, bass.ds(t, 1)]).then_inc(s_yo, 1)

            act.wait_ge(s_et, 1)

            def step(t, par, first=False, last=False):
                e = act.value_load(etile[0:1, bass.ds(t, 1)], min_val=0, max_val=E - 1)
                relu(t, 0, e)
                if not last:
                    tile_hi(t + 1, 1 - par)
                relu(t, 1, e)
                if not first:
                    gate_y(t - 1, 1 - par)

            tile_hi(0, 0)
            step(0, 0, first=True)
            step(1, 1)
            with act.Fori(2, TILES - 1, 2) as i:
                for par in range(2):
                    step(i + par, par)
            step(TILES - 1, 0, last=True)
            gate_y(TILES - 1, 0)

        @block.tensor
        def _(pe):
            pe.wait_ge(s_cst, 32)
            pe.wait_ge(s_par, 16 * 12)
            nc.tensor.transpose(bk_small[:, 0:VEC_ROWS], vrows[0:VEC_ROWS, :], ident[0:VEC_ROWS, 0:VEC_ROWS]).then_inc(s_small_pe, 1)
            def transposes(b, par):
                pe.wait_ge(s_xn, b + 1)
                if not (isinstance(b, int) and b == 0):
                    pe.wait_ge(s_hT, b)
                for k in range(KD):
                    for j in range(JB):
                        ins = nc.tensor.transpose(bk_T[k][:, j * P:(j + 1) * P], xn[:, par, j * D + k * P:j * D + (k + 1) * P], ident)
                ins.then_inc(s_tr, 1)

            def back(b, par):
                pe.wait_ge(s_h2, b + 1)
                if not (isinstance(b, int) and b == 0):
                    pe.wait_ge(s_hrow, b)
                for j in range(JB):
                    for k in range(KD):
                        at = (j % 2) * D + k * P
                        ins = nc.tensor.transpose(bk_back[j // 2][:, at:at + P], h2T[:, par, k * T + j * P:k * T + (j + 1) * P], ident)
                ins.then_inc(s_back, 1)
                if not (isinstance(b, int) and b < 2):
                    pe.wait_ge(s_lgc, b - 1)
                for j in range(JB):
                    for k in range(KD):
                        ins = nc.tensor.matmul(bk_log[par][:, j * E:(j + 1) * E], h2T[:, par, k * T + j * P:k * T + (j + 1) * P],
                                               rw[:, k * E:(k + 1) * E], start=(k == 0), stop=(k == KD - 1))
                ins.then_inc(s_log, 1)

            transposes(0, 0)
            transposes(1, 1)
            pe.wait_ge(s_se, 16)
            nc.tensor.transpose(bk_cnt[0:SE, 0:B], se[:, :], ident[0:B, 0:B]).then_inc(s_small_pe, 1)
            pe.wait_ge(s_small_v, 2)
            nc.tensor.matmul(bk_small[:, 0:B], hw1[:, :], sT[0:SE, 0, :], start=True, stop=True).then_inc(s_small_pe, 1)
            pe.wait_ge(s_small_v, 3)
            nc.tensor.matmul(bk_cnt[:, 0:B], hw2[:, :], sT[:, 1, :], start=True, stop=True).then_inc(s_small_pe, 1)
            pe.wait_ge(s_small_v, 4)
            nc.tensor.matmul(bk_small[0:SH // 2, 0:B], sw1[:, :], sT[:, 2, :], start=True, stop=True).then_inc(s_small_pe, 1)
            pe.wait_ge(s_small_v, 5)
            for c in range(4):
                ins = nc.tensor.matmul(bk_cnt[:, c * B:(c + 1) * B], sw2[:, c * P:(c + 1) * P], sT[0:SH // 2, 3, :], start=True, stop=True)
            ins.then_inc(s_small_pe, 1)
            back(0, 0)
            transposes(2, 0)
            back(1, 1)
            with pe.Fori(3, B - 1, 2) as i:
                transposes(i, 1)
                back(i - 1, 0)
                transposes(i + 1, 0)
                back(i, 1)
            transposes(B - 1, 1)
            back(B - 2, 0)
            back(B - 1, 1)

            pe.wait_ge(s_sel, 1)
            nc.tensor.matmul(bk_cnt[:, 0:NBLK], ones16, selh[:, 1:NBLK + 1], start=True, stop=True).then_inc(s_cnt, 1)
            pe.wait_ge(s_ds, 1)
            for h in range(NH):
                ins = nc.tensor.matmul(bk_small[:, h * P:(h + 1) * P], dsel[:, h * P:(h + 1) * P], upto, start=True, stop=True)
            ins.then_inc(s_dp, 1)

            def slot_table(t, par):
                pe.wait_ge(s_step, t + 1)
                if not (isinstance(t, int) and t == 0):
                    pe.wait_ge(s_tok, t)
                for h in range(NH):
                    ins = nc.tensor.matmul(bk_tab[:, 0:P + 2], step16[:, par, h, :], table[:, h, :], start=(h == 0), stop=(h == NH - 1))
                ins.then_inc(s_tab, 1)

            def tile_transpose(t, par):
                if isinstance(t, int):
                    pe.wait_ge(s_gh[par], 16 * (t // 2 + 1))
                else:
                    pe.wait_ge(s_gh[par], (t - par) * 8 + 16)
                if not (isinstance(t, int) and t == 0):
                    pe.wait_ge(s_lo, t)
                for k in range(KD):
                    ins = nc.tensor.transpose(bk_g[:, k * P:(k + 1) * P], hg[:, par, k * P:(k + 1) * P], ident)
                ins.then_inc(s_gt, 1)

            def hidden(t, par, half, e):
                if half == 0:
                    pe.wait_ge(s_hi, t + 1)
                    pe.wait_ge(s_lo, t + 1)
                if not (isinstance(t, int) and t == 0):
                    pe.wait_ge(s_relu, 2 * t + half - 1)
                for c in range(4 * half, 4 * half + 4):
                    o = bk_hid[half][:, (c - 4 * half) * P:(c - 4 * half + 1) * P]
                    n = 0
                    for w, parts in ((whi, (hThi, hTlo)), (wlo, (hThi,))):
                        for k in range(KD):
                            lhs = w[:, bass.ds(e * (2 * UNIT) + k * FF + c * P, P)]
                            for h in parts:
                                ins = nc.tensor.matmul(o, lhs, h[:, par, k * P:(k + 1) * P], start=(n == 0), stop=(n == 3 * KD - 1))
                                n += 1
                ins.then_inc(s_hm, 1)

            def output(t, par, e):
                pe.wait_ge(s_split, 2 * t + 2)
                if not (isinstance(t, int) and t < 2):
                    pe.wait_ge(s_ys, t - 1)
                n = 0
                for c in range(FC):
                    for h, ws in ((hidhi, (whi, wlo)), (hidlo, (whi,))):
                        for w in ws:
                            ins = nc.tensor.matmul(bk_y[par][:, 0:D], h[:, par, c * P:(c + 1) * P], w[:, bass.ds(e * (2 * UNIT) + UNIT + c * D, D)],
                                                   start=(n == 0), stop=(n == 3 * FC - 1))
                            n += 1
                ins.then_inc(s_ym, 1)

            for t in range(3):
                slot_table(t, t % 2)
            pe.wait_ge(s_et, 1)
            pe.wait_ge(s_whi, UNITS)
            for slot in range(NSTAGE):
                pe.wait_ge(s_wlo[slot], len(range(slot, UNITS, NSTAGE)))

            def expert(t):
                return pe.value_load(etile[0:1, bass.ds(t, 1)], min_val=0, max_val=E - 1)

            def step(t, par, first=False, last=0):
                e = expert(t)
                hidden(t, par, 0, e)
                if last < 1:
                    tile_transpose(t + 1, 1 - par)
                if last < 1 or last == 3:
                    slot_table(t + 3, 1 - par)
                hidden(t, par, 1, e)
                if not first:
                    output(t - 1, 1 - par, expert(t - 1))

            tile_transpose(0, 0)
            step(0, 0, first=True)
            step(1, 1)
            with pe.Fori(2, TILES - 3, 2) as i:
                for par in range(2):
                    step(i + par, par)
            for t in range(TILES - 3, TILES):
                e = expert(t)
                hidden(t, t % 2, 0, e)
                if t + 1 < TILES:
                    tile_transpose(t + 1, (t + 1) % 2)
                hidden(t, t % 2, 1, e)
                output(t - 1, (t - 1) % 2, expert(t - 1))
            output(TILES - 1, 0, expert(TILES - 1))

        @block.vector
        def _(ve):
            links = [0]

            def link(ins):
                links[0] += 1
                ins.then_inc(s_v, 1)
                ve.wait_ge(s_v, links[0])

            V = nc.vector
            link(V.memset(selh[:, 0:1], 0.0))
            link(V.memset(start[:, 0:1], 0.0))
            ve.wait_ge(s_small_pe, 1)
            V.tensor_copy(vcol[:, :], bk_small[:, 0:VEC_ROWS]).then_inc(s_small_v, 1)
            gam_v = gam[:, :].rearrange("p (k b) -> p b k", k=KD)
            bet_v = bet[:, :].rearrange("p (k b) -> p b k", k=KD)

            s_vb = s_dv

            def token_stats(b, par, at):
                if isinstance(b, int):
                    ve.wait_ge(s_x[par], b // 2 * 16 + 16)
                else:
                    ve.wait_ge(s_x[par], (b - par) * 8 + 16)
                for j in range(JB):
                    ins = V.bn_stats(bns[:, j, :], xs[:, par, j * D:(j + 1) * D])
                ins.then_inc(s_vb, 1)
                ve.wait_ge(s_vb, at + 1)
                ve.memset(held_ve[:, :], 0.0)
                for j in range(JB):
                    ins = V.bn_aggr(mv[:, par, j, :], bns[:, j, :])
                ins.then_inc(s_vb, 1)
                ve.wait_ge(s_vb, at + 2)
                V.tensor_scalar(lnv[:, par, 0, :], mv[:, par, :, 1], LN_EPS, None, ALU.add).then_inc(s_lnv, 1)

            def token_norm(b, par, at):
                ve.wait_ge(s_sd, b + 1)
                V.reciprocal(lnv[:, par, 2, :], lnv[:, par, 1, :]).then_inc(s_vb, 1)
                ve.wait_ge(s_vb, at + 1)
                V.scalar_tensor_tensor(out=lnv[:, par, 3, :], in0=mv[:, par, :, 0], scalar=-1.0, in1=lnv[:, par, 2, :],
                                       op0=ALU.mult, op1=ALU.mult).then_inc(s_nrm, 1)

            def time_stats(b, par, at):
                ve.wait_ge(s_hT, b + 1)
                for k in range(KD):
                    ins = V.bn_stats(tns[:, k, :], hT[:, par, k * T:(k + 1) * T])
                ins.then_inc(s_vb, 1)
                ve.wait_ge(s_vb, at + 1)
                ve.memset(held_ve[:, :], 0.0)
                for k in range(KD):
                    ins = V.bn_aggr(tmv[:, par, k, :], tns[:, k, :])
                ins.then_inc(s_vb, 1)
                ve.wait_ge(s_vb, at + 2)
                V.tensor_scalar(tnv[:, par, 0, :], tmv[:, par, :, 1], T_EPS, None, ALU.add).then_inc(s_tst, 1)

            def modulate(b, par, at):
                ve.wait_ge(s_tsd, b + 1)
                V.reciprocal(tnv[:, par, 2, :], tnv[:, par, 1, :]).then_inc(s_vb, 1)
                ve.wait_ge(s_vb, at + 1)
                g_b = gam_v[:, bass.ds(b, 1), :].rearrange("p b k -> p (b k)")
                e_b = bet_v[:, bass.ds(b, 1), :].rearrange("p b k -> p (b k)")
                V.tensor_tensor(tnv[:, par, 3, :], tnv[:, par, 2, :], g_b, ALU.mult).then_inc(s_vb, 1)
                ve.wait_ge(s_vb, at + 2)
                V.tensor_tensor(tnv[:, par, 4, :], tmv[:, par, :, 0], tnv[:, par, 3, :], ALU.mult).then_inc(s_vb, 1)
                ve.wait_ge(s_vb, at + 3)
                V.tensor_tensor(tnv[:, par, 5, :], e_b, tnv[:, par, 4, :], ALU.subtract).then_inc(s_vb, 1)
                ve.wait_ge(s_vb, at + 4)
                if not (isinstance(b, int) and b < 2):
                    ve.wait_ge(s_log, b - 1)
                for k in range(KD):
                    ins = V.tensor_scalar(h2T[:, par, k * T:(k + 1) * T], hT[:, par, k * T:(k + 1) * T],
                                          tnv[:, par, 3, k:k + 1], tnv[:, par, 5, k:k + 1], ALU.mult, ALU.add)
                ins.then_inc(s_h2, 1)

            def copy_logits(b, par):
                ve.wait_ge(s_log, b + 1)
                V.tensor_copy(lg[:, bass.ds(b * JB * E, JB * E)], bk_log[par][:, 0:JB * E]).then_inc(s_lgc, 1)

            L = 9
            token_stats(0, 0, 0)
            token_norm(0, 0, 2)
            token_stats(1, 1, 3)
            token_norm(1, 1, 5)
            time_stats(0, 0, 6)
            ve.wait_ge(s_small_pe, 2)
            V.tensor_copy(sT[0:SE, 0, :], bk_cnt[0:SE, 0:B]).then_inc(s_small_v, 1)
            ve.wait_ge(s_small_v, 2)
            ve.wait_ge(s_small_pe, 3)
            V.tensor_scalar(sT[:, 1, :], bk_small[:, 0:B], vcol[:, V_HB1:V_HB1 + 1], 0.0, ALU.add, ALU.max).then_inc(s_small_v, 1)
            ve.wait_ge(s_small_pe, 4)
            V.tensor_scalar(sT[:, 2, :], bk_cnt[:, 0:B], vcol[:, V_HB2:V_HB2 + 1], None, ALU.add).then_inc(s_small_v, 1)
            ve.wait_ge(s_small_pe, 5)
            V.tensor_scalar(sT[0:SH // 2, 3, :], bk_small[0:SH // 2, 0:B], vcol[0:SH // 2, V_SB1:V_SB1 + 1], 0.0, ALU.add, ALU.max).then_inc(s_small_v, 1)
            ve.wait_ge(s_small_pe, 6)
            for c in range(4):
                dst = (gam, bet)[c // 2][:, (c % 2) * B:(c % 2 + 1) * B]
                V.tensor_scalar(dst, bk_cnt[:, c * B:(c + 1) * B], vcol[:, V_SB2 + c:V_SB2 + c + 1], None, ALU.add).then_inc(s_small_v, 1)
            ve.wait_ge(s_small_v, 9)
            link(V.scalar_tensor_tensor(out=sp[:, 0, :], in0=gam[:, :], scalar=-1.0, in1=gam[:, :], op0=ALU.mult, op1=ALU.min))
            V.tensor_scalar(sp[:, 1, :], sp[:, 0, :], 0.0, None, ALU.min).then_inc(s_small_v, 1)
            ve.wait_ge(s_small_a, 1)
            V.tensor_scalar(sp[:, 3, :], sp[:, 2, :], 1.0, None, ALU.add).then_inc(s_small_v, 1)
            ve.wait_ge(s_small_v, 11)
            link(V.tensor_scalar(sp[:, 0, :], sp[:, 3, :], -1.0, None, ALU.add))
            link(V.tensor_scalar(sp[:, 1, :], sp[:, 0, :], 0.0, None, ALU.is_equal))
            link(V.tensor_scalar(sp[:, 5, :], sp[:, 0, :], 1e-30, None, ALU.max))
            ve.wait_ge(s_small_a, 2)
            link(V.reciprocal(sp[:, 3, :], sp[:, 5, :]))
            link(V.tensor_tensor(sp[:, 5, :], sp[:, 4, :], sp[:, 3, :], ALU.mult))
            link(V.tensor_tensor(sp[:, 0, :], sp[:, 5, :], sp[:, 1, :], ALU.add))
            link(V.tensor_tensor(sp[:, 3, :], sp[:, 0, :], sp[:, 2, :], ALU.mult))
            link(V.scalar_tensor_tensor(out=sp[:, 5, :], in0=gam[:, :], scalar=0.0, in1=sp[:, 3, :], op0=ALU.max, op1=ALU.add))
            link(V.tensor_scalar(gam[:, :], sp[:, 5, :], T_EPS, None, ALU.add))

            def w_lo(g, slot):
                at = g * (NSTAGE * UNIT) + slot * UNIT
                ve.wait_ge(s_whi, g * NSTAGE + slot + 1)
                V.scalar_tensor_tensor(out=wlo[:, bass.ds(at, UNIT)], in0=stage[:, slot, :], scalar=WSCALE,
                                       in1=whi[:, bass.ds(at, UNIT)], op0=ALU.mult, op1=ALU.subtract).then_inc(s_wlo[slot], 1)

            def batch(b, par, at):
                token_stats(b, par, at)
                modulate(b - 2, par, at + 2)
                token_norm(b, par, at + 6)
                time_stats(b - 1, 1 - par, at + 7)
                copy_logits(b - 2, par)

            batch(2, 0, 8)
            w_lo(0, 0)
            batch(3, 1, 8 + L)
            w_lo(0, 1)
            w_lo(0, 2)
            with ve.Fori(2, B // 2) as g:
                for par in range(2):
                    batch(g * 2 + par, par, g * (2 * L) + (par - 2) * L + 8)
                    w_lo(g - 1, par)
                w_lo(g - 1, 2)
            at = (B - 2) * L + 8
            modulate(B - 2, 0, at)
            time_stats(B - 1, 1, at + 4)
            modulate(B - 1, 1, at + 6)
            copy_logits(B - 2, 0)
            copy_logits(B - 1, 1)
            vb_end = at + 10

            def by_expert(a):
                return a.rearrange("p (j e) -> p j e", e=E)

            def over(a):
                return a.unsqueeze(2).broadcast_to([P, NJ, E])

            desc_b = desc.unsqueeze(1).broadcast_to([P, NJ, E])
            lg3, d13, d23, ex3, oh13, tm3 = (by_expert(a[:, :]) for a in (lg, d1, d2, ex, oh1, tm))
            ve.wait_ge(s_lgc, B)
            link(V.memset(ones[:, :], 1.0))
            link(V.tensor_reduce(m8[:, 0, :], lg3, AX_X, ALU.max))
            V.tensor_tensor(d13, lg3, over(m8[:, 0, :]), ALU.subtract).then_inc(s_d, 1)
            ve.wait_ge(s_d, 1)
            link(V.scalar_tensor_tensor(out=tm3, in0=d13, scalar=0.0, in1=desc_b, op0=ALU.is_ge, op1=ALU.mult))
            link(V.tensor_reduce(m8[:, 1, :], tm3, AX_X, ALU.max))
            link(V.tensor_tensor(oh13, desc_b, over(m8[:, 1, :]), ALU.is_equal))
            link(V.scalar_tensor_tensor(out=d2[:, :], in0=oh1[:, :], scalar=-3e38, in1=d1[:, :], op0=ALU.mult, op1=ALU.add))
            link(V.tensor_reduce(m8[:, 2, :], d23, AX_X, ALU.max))
            link(V.tensor_tensor(tm3, d23, over(m8[:, 2, :]), ALU.is_ge))
            link(V.tensor_tensor(d23, tm3, desc_b, ALU.mult))
            link(V.tensor_reduce(m8[:, 3, :], d23, AX_X, ALU.max))
            link(V.tensor_tensor(tm3, desc_b, over(m8[:, 3, :]), ALU.is_equal))
            link(V.tensor_tensor(d2[:, :], tm[:, :], oh1[:, :], ALU.add))
            V.tensor_copy(selh[:, 1:NBLK + 1].rearrange("p (e j) -> p j e", e=E), d23).then_inc(s_sel, 1)
            ve.wait_ge(s_sel, 1)
            V.tensor_tensor(dsel[:, :], selh[:, 1:NBLK + 1], selh[:, 0:NBLK], ALU.subtract).then_inc(s_ds, 1)

            ve.wait_ge(s_cnt, 1)
            cnt = bk_cnt[:, 0:NBLK]
            link(V.tensor_tensor_scan(csum[:, :], ones[:, :], cnt, 0.0, ALU.mult, ALU.add))
            link(V.tensor_reduce(ne[:, 0, :], cnt.rearrange("p (e j) -> p e j", e=E), AX_X, ALU.add))
            link(V.tensor_scalar(nei[:, 0, :], ne[:, 0, :], float(P - 1), None, ALU.add))
            link(V.tensor_single_scalar(nei[:, 1, :], nei[:, 0, :], -P, ALU.bitwise_and))
            link(V.tensor_copy(ne[:, 1, :], nei[:, 1, :]))
            link(V.tensor_tensor_scan(ne[:, 2, :], ones[:, 0:E], ne[:, 1, :], 0.0, ALU.mult, ALU.add))
            link(V.tensor_tensor(ne[:, 3, :], ne[:, 2, :], ne[:, 1, :], ALU.subtract))
            link(V.tensor_tensor(ne[:, 4, :], csum[:, :].rearrange("p (e j) -> p e j", e=E)[:, :, NJ - 1], ne[:, 0, :], ALU.subtract))
            link(V.tensor_tensor(ne[:, 5, :], ne[:, 3, :], ne[:, 4, :], ALU.subtract))
            link(V.tensor_tensor(dstart[:, :], csum[:, :], cnt, ALU.subtract))
            link(V.tensor_tensor(start[:, 1:NBLK + 1].rearrange("p (e j) -> p e j", e=E), dstart[:, :].rearrange("p (e j) -> p e j", e=E),
                                 ne[:, 5, :].unsqueeze(2).broadcast_to([P, E, NJ]), ALU.add))
            link(V.tensor_tensor(dstart[:, :], start[:, 1:NBLK + 1], start[:, 0:NBLK], ALU.subtract))
            for h in range(NH):
                V.tensor_tensor_reduce(tm[:, 0:P], start[:, 1 + h * P:1 + (h + 1) * P], ident, 1.0, 0.0, ALU.mult, ALU.add,
                                       stcol[:, h:h + 1])
                ins = V.tensor_tensor_reduce(tm[:, P:2 * P], dstart[:, h * P:(h + 1) * P], ident, 1.0, 0.0, ALU.mult, ALU.add,
                                             stcol[:, NH + h:NH + h + 1])
                link(ins)
            ve.wait_ge(s_dp, 1)
            for h in range(NH):
                V.tensor_scalar(table[:, h, 0:P], bk_small[:, h * P:(h + 1) * P], stcol[:, NH + h:NH + h + 1], None, ALU.add)
                link(V.tensor_copy(table[:, h, P:P + 2], cst[:, C_DJ + 2 * h:C_DJ + 2 * h + 2]))

            t128 = cst[:, C_T128:C_T128 + 72].unsqueeze(2).broadcast_to([P, 72, E])
            ge3 = ge[:, :].rearrange("p (t e) -> p t e", e=E + 1)
            ohe3 = ohe[:, :].rearrange("p (t e) -> p t e", e=E)
            ve.wait_ge(s_hst[0], 16 * (B // 2))
            link(V.memset(ge3[:, :, E:E + 1], 0.0))
            link(V.tensor_tensor(ge3[:, :, 0:E], t128, ne[:, 3, :].unsqueeze(1).broadcast_to([P, 72, E]), ALU.is_ge))
            link(V.tensor_tensor(ohe3, ge3[:, :, 0:E], ge3[:, :, 1:E + 1], ALU.subtract))
            link(V.tensor_reduce(tm[:, 0:72], ge3[:, :, 0:E], AX_X, ALU.add))
            V.tensor_scalar(etile[:, :], tm[:, 0:72], -1.0, None, ALU.add).then_inc(s_et, 1)

            def slot_steps(t, par):
                if not (isinstance(t, int) and t < 2):
                    ve.wait_ge(s_tab, t - 1)
                for h in range(NH):
                    ins = V.tensor_scalar(step16[:, par, h, :], slotrow, stcol[:, h:h + 1], cst[:, bass.ds(t + C_NEGT, 1)],
                                          ALU.subtract, ALU.is_ge)
                ins.then_inc(s_step, 1)

            def slot_tokens(t, par, at):
                ve.wait_ge(s_tab, t + 1)
                if not (isinstance(t, int) and t < 2):
                    n = t // 2 * 16 if isinstance(t, int) else (t - par) * 8
                    ve.wait_ge(s_gh[par], n)
                    ve.wait_ge(s_gc[par], n)
                V.tensor_scalar(junk, bk_tab[:, 0:P], cst[:, bass.ds(t + C_SLOTCOL, 1)], None, ALU.is_le).then_inc(s_dv, 1)
                V.tensor_tensor_reduce(rj[:, :], bk_tab[:, P:P + 2], cst[:, C_TOK2:C_TOK2 + 2], 1.0, 0.0,
                                       ALU.mult, ALU.add, rt[:, par, 1:2]).then_inc(s_dv, 1)
                ve.wait_ge(s_dv, at + 2)
                V.tensor_reduce(rt[:, par, 0:1], junk, AX_X, ALU.add).then_inc(s_dv, 1)
                ve.wait_ge(s_dv, at + 3)
                V.tensor_scalar(rt[:, par, 2:3], rt[:, par, 0:1], float(P), qcol, ALU.is_ge, ALU.mult)
                V.scalar_tensor_tensor(out=rt[:, par, 3:4], in0=rt[:, par, 0:1], scalar=float(JB), in1=rt[:, par, 1:2],
                                       op0=ALU.mult, op1=ALU.add).then_inc(s_dv, 1)
                ve.wait_ge(s_dv, at + 4)
                V.tensor_tensor(idxg[par][:, :], rt[:, par, 2:3], rt[:, par, 3:4], ALU.add)
                V.tensor_tensor(tok[:, bass.ds(t, 1)], rt[:, par, 2:3], rt[:, par, 3:4], ALU.add).then_inc(s_tok, 1)

            def gate(t, par, at):
                if isinstance(t, int):
                    ve.wait_ge(s_gc[par], 16 * (t // 2 + 1))
                else:
                    ve.wait_ge(s_gc[par], (t - par) * 8 + 16)
                V.tensor_tensor(gprod[:, par, :], cg[:, par, :], ohe[:, bass.ds(t * E, E)], ALU.mult).then_inc(s_dv, 1)
                ve.wait_ge(s_dv, at + 1)
                V.tensor_reduce(gates[:, bass.ds(t, 1)], gprod[:, par, :], AX_X, ALU.add).then_inc(s_gate, 1)

            def tile_lo(t, par):
                ve.wait_ge(s_hi, t + 1)
                V.tensor_tensor(hTlo[:, par, :], bk_g[:, 0:D], hThi[:, par, :], ALU.subtract).then_inc(s_lo, 1)

            def split(t, par, half, at):
                ve.wait_ge(s_relu, 2 * t + half + 1)
                if half == 0 and not (isinstance(t, int) and t < 2):
                    ve.wait_ge(s_ym, t - 1)
                a, b = half * 512, half * 512 + 512
                V.tensor_copy(hidhi[:, par, a:b], hid32[:, a:b]).then_inc(s_dv, 1)
                ve.wait_ge(s_dv, at + 1)
                V.tensor_tensor(hidlo[:, par, a:b], hid32[:, a:b], hidhi[:, par, a:b], ALU.subtract).then_inc(s_split, 1)

            def bias_y(t, par, e):
                ve.wait_ge(s_ym, t + 1)
                if not (isinstance(t, int) and t < 2):
                    ve.wait_ge(s_yo, t - 1)
                V.scalar_tensor_tensor(out=ysum[:, par, :], in0=bk_y[par][:, 0:D], scalar=1.0 / WSCALE,
                                       in1=b2row[:, bass.ds(e * D, D)], op0=ALU.mult, op1=ALU.add).then_inc(s_ys, 1)

            ve.wait_ge(s_exp, 1)
            link(V.tensor_reduce(m8[:, 4, :], ex3, AX_X, ALU.add))
            link(V.reciprocal(m8[:, 5, :], m8[:, 4, :]))
            link(V.tensor_tensor(ex3, ex3, over(m8[:, 5, :]), ALU.mult))
            link(V.tensor_tensor(tm[:, :], ex[:, :], d2[:, :], ALU.mult))
            link(V.tensor_reduce(m8[:, 6, :], tm3, AX_X, ALU.add))
            link(V.reciprocal(m8[:, 7, :], m8[:, 6, :]))
            V.tensor_tensor(oh13, tm3, over(m8[:, 7, :]), ALU.mult).then_inc(s_comb, 1)

            for u in range(NSTAGE * (B // 2 - 1), UNITS):
                w_lo(u // NSTAGE, u % NSTAGE)

            at = vb_end
            slot_steps(0, 0)
            slot_steps(1, 1)
            for t in range(3):
                slot_tokens(t, t % 2, at)
                at += 4
                if t < 2:
                    slot_steps(t + 2, t % 2)
            for t in range(2):
                gate(t, t % 2, at)
                at += 1
            tile_lo(0, 0)
            ve.wait_ge(s_b2, 16)

            def vexpert(t):
                return ve.value_load(etile[0:1, bass.ds(t, 1)], min_val=0, max_val=E - 1)

            def step(t, par, at, first=False, left=9):
                split(t, par, 0, at)
                if left > 0:
                    tile_lo(t + 1, 1 - par)
                split(t, par, 1, at + 1)
                n = 2
                if left > 2:
                    slot_tokens(t + 3, 1 - par, at + n)
                    n += 4
                if left > 3:
                    slot_steps(t + 4, par)
                if left > 1:
                    gate(t + 2, par, at + n)
                    n += 1
                if not first:
                    bias_y(t - 1, 1 - par, vexpert(t - 1))
                return n

            base = at
            LT = step(0, 0, base, first=True)
            step(1, 1, base + LT)
            with ve.Fori(2, TILES - 5, 2) as i:
                for par in range(2):
                    step(i + par, par, (i + par) * LT + base)
            at = (TILES - 5) * LT + base
            for t in range(TILES - 5, TILES):
                at += step(t, t % 2, at, left=TILES - 1 - t)
            bias_y(TILES - 1, 0, vexpert(TILES - 1))


def constants():
    import numpy as np

    c = np.zeros((P, C_END), np.float32)
    q = np.arange(P)
    c[:, C_ID:C_ID + P] = np.eye(P)
    c[:, C_SLOT:C_SLOT + P] = q
    t = np.arange(72)
    c[:, C_NEGT:C_NEGT + 72] = -P * t
    c[:, C_SLOTCOL:C_SLOTCOL + 72] = P * t + q[:, None]
    c[:, C_Q] = q
    pair = np.arange(NBLK)
    for i, v in enumerate((pair % NJ // JB, pair % JB)):
        step = np.diff(v, prepend=0)
        for h in range(NH):
            c[:, C_DJ + 2 * h + i] = step[h * P:(h + 1) * P]
    c[:, C_DESC:C_DESC + E] = E - np.arange(E)
    c[:, C_TOK2] = T
    c[:, C_TOK2 + 1] = 1
    c[:, C_T128:C_T128 + 72] = P * t
    c16 = np.ones((P, 2 * P), np.float16)
    c16[:, 0:P] = q[:, None] <= q
    return c, c16


_INS = ["x", "itok_B_6_14"] + ["L0_cond_" + n for n in (
    "ln_g", "ln_b", "subj_emb", "hyp_w1", "hyp_b1", "hyp_w2", "hyp_b2", "sty_w1", "sty_b1", "sty_w2", "sty_b2",
    "router_w", "exp_w1", "exp_b1", "exp_w2", "exp_b2")]


def kernel(**inputs):
    import numpy as np
    import concourse.bacc as bacc
    from concourse.bass_utils import run_bass_kernel_spmd

    nc = bacc.Bacc("TRN2", target_bir_lowering=False, num_devices=1)
    arrays, args = {}, []
    named = [(n, np.ascontiguousarray(inputs[n])) for n in _INS] + list(zip(("consts", "consts16"), constants()))
    for name, a in named:
        arrays[f"in_{name}"] = a
        args.append(nc.dram_tensor(f"in_{name}", a.shape, mybir.dt.from_np(a.dtype), kind="ExternalInput").ap())
    args.append(nc.dram_tensor("out_rows", (ROWS, D), F32, kind="ExternalOutput").ap())
    moe_kernel(nc, *args)
    r = run_bass_kernel_spmd(nc, [arrays], core_ids=[0])
    return r.results[0]["out_rows"][:N].reshape(B, T, D)
```

```python
from contextlib import ExitStack

import concourse.bass as bass
from concourse import mybir

F32 = mybir.dt.float32
F16 = mybir.dt.float16
I32 = mybir.dt.int32
ALU = mybir.AluOpType
ACT = mybir.ActivationFunctionType
AX_X = mybir.AxisListType.X

P = 128
B, T, D = 8, 512, 256
E, FF = 8, 1024
NSUBJ, SE, SH = 32, 64, 128
N = B * T
KD = D // P
FC = FF // P
JB = T // P
NJ = N // P
NBLK = E * NJ
NH = NBLK // P
TILES = (2 * N + E * (P - 1)) // P
ROWS = N + P + 8
HROW = D + E
WSCALE = 64.0
LN_EPS, T_EPS = 1e-5, 1e-8
UNIT = 2 * FF
UNITS = 2 * E
NSTAGE = 4
VEC_ROWS = 75
V_LNG, V_LNB, V_HB1, V_HB2, V_SB1, V_SB2 = 64, 66, 68, 69, 70, 71

C_ID, C_SLOT, C_NEGT, C_SLOTCOL, C_Q, C_DJ, C_DESC, C_TOK2, C_T128 = 0, 128, 256, 328, 400, 401, 405, 413, 415
C_END = C_T128 + 72


def moe_kernel(nc, x, ids, ln_g, ln_b, subj_emb, hyp_w1, hyp_b1, hyp_w2, hyp_b2, sty_w1, sty_b1,
               sty_w2, sty_b2, router_w, exp_w1, exp_b1, exp_w2, exp_b2, consts, consts16, out):
    h_dram = nc.dram_tensor("h_rows", (ROWS, HROW), F32).ap()
    x_v = x.rearrange("b (p j) d -> b p (j d)", j=JB)
    out_v = out[0:N, :].rearrange("(b p j) d -> b p (j d)", b=B, j=JB)
    h_v = h_dram[0:N, 0:D].rearrange("(b p j) d -> b p j d", b=B, j=JB)
    comb_v = h_dram[0:N, D:HROW].rearrange("(b p j) e -> b p j e", b=B, j=JB)
    w1_v = exp_w1.rearrange("e (k p) f -> e p k f", p=P)
    w2_v = exp_w2.rearrange("e (c p) d -> e p c d", p=P)

    def w_v(u):
        return (w2_v if u % 2 else w1_v)[u // 2]

    with ExitStack() as ctx:
        def sb(name, shape, dt=F32):
            return ctx.enter_context(nc.sbuf_tensor(name, shape, dt))

        def sem(name):
            return ctx.enter_context(nc.semaphore(name))

        whi = sb("whi", [P, UNITS * UNIT], F16)
        wlo = sb("wlo", [P, UNITS * UNIT], F16)
        stage = sb("stage", [P, NSTAGE, UNIT])
        cst = sb("cst", [P, C_END])
        c16 = sb("c16", [P, 2 * P], F16)

        xs = sb("xs", [P, 2, JB * D])
        xn = sb("xn", [P, 2, JB * D])
        hT = sb("hT", [P, 2, KD * T])
        hrow = sb("hrow", [P, 2, JB * D])
        hid32 = stage[:, 0, 0:FF]
        hidhi = stage[:, 1, 0:FF].bitcast(F16).rearrange("p (a f) -> p a f", a=2)
        hidlo = stage[:, 2, 0:FF].bitcast(F16).rearrange("p (a f) -> p a f", a=2)
        b2row = hrow[:, :, :].rearrange("p a n -> p (a n)")
        hg = xs[:, 0, 0:2 * HROW].rearrange("p (a d) -> p a d", a=2)
        ysum = xn[:, 0, 2 * D:4 * D].rearrange("p (a d) -> p a d", a=2)
        yout = xs[:, 1, 0:2 * D].rearrange("p (a d) -> p a d", a=2)
        hThi = xn[:, 0, 0:D].bitcast(F16).rearrange("p (a d) -> p a d", a=2)
        hTlo = xn[:, 0, D:2 * D].bitcast(F16).rearrange("p (a d) -> p a d", a=2)
        step16 = xn[:, 1, 0:2 * P].bitcast(F16).rearrange("p (a h s) -> p a h s", a=2, h=NH)
        junk = xn[:, 1, 2 * P:3 * P]

        hw1 = hrow[0:SE, 1, 0:SH]
        hw2 = hrow[:, 1, SH:2 * SH]
        sw1 = hrow[:, 1, 2 * SH:2 * SH + SH // 2]
        sw2 = hrow[0:SH // 2, 1, 320:320 + 2 * D]
        d1, d2, ex, oh1 = (hT[:, 1, i * NBLK:(i + 1) * NBLK] for i in range(4))
        tm = xn[:, 1, 3 * P:5 * P]
        csum, dstart = xn[:, 0, 2 * D:3 * D], xn[:, 0, 3 * D:4 * D]
        ones = xs[:, 0, 3 * D:4 * D]
        ge = xs[:, 1, 0:72 * E]

        vrows = sb("vrows", [P, P])
        vcol = sb("vcol", [P, VEC_ROWS])
        rw = sb("rw", [P, KD * E])
        idcol = sb("idcol", [B, 1], I32)
        se = sb("se", [B, SE])
        sT = sb("sT", [P, 4, B])
        gam = sb("gam", [P, KD * B])
        bet = sb("bet", [P, KD * B])
        sp = sb("sp", [P, 6, KD * B])
        bns = sb("bns", [P, JB, 6])
        mv = sb("mv", [P, 2, JB, 2])
        lnv = sb("lnv", [P, 2, 4, JB])
        tns = sb("tns", [P, KD, 6])
        tmv = sb("tmv", [P, 2, KD, 2])
        tnv = sb("tnv", [P, 2, 6, KD])
        lg = sb("lg", [P, NJ * E])
        selh = sb("selh", [P, NBLK + 1], F16)
        dsel = sb("dsel", [P, NBLK], F16)
        m8 = sb("m8", [P, 8, NJ])
        start = sb("start", [P, NBLK + 1])
        ne = sb("ne", [P, 6, E])
        nei = sb("nei", [P, 2, E], I32)
        stcol = sb("stcol", [P, 2 * NH])
        table = sb("table", [P, NH, P + 2], F16)
        etile = sb("etile", [P, 72], I32)
        tok = sb("tok", [P, 72], I32)
        gates = sb("gates", [P, 72])
        epairs = sb("epairs", [P, 36, 4], I32)
        rt = sb("rt", [P, 2, 4])
        rj = sb("rj", [P, 2])
        idxg = [sb(f"idxg{i}", [P, 1], I32) for i in range(2)]
        idxs = [sb(f"idxs{i}", [P, 1], I32) for i in range(2)]
        zero = sb("zero", [P, HROW])
        held_gp = sb("held_gp", [1, 2])
        held_ve = sb("held_ve", [1, 1])

        banks = [ctx.enter_context(nc.psum_tensor(f"bank{i}", [P, 512], F32)) for i in range(8)]
        bk_T = banks[0:2]
        bk_back = banks[2:4]
        bk_log = banks[4:6]
        bk_small = banks[6]
        bk_cnt = banks[7]
        bk_hid = banks[0:2]
        bk_y = banks[2:4]
        bk_g = banks[4]
        bk_tab = banks[5]

        ident = cst[:, C_ID:C_ID + P]
        slotrow = cst[:, C_SLOT:C_SLOT + P]
        desc = cst[:, C_DESC:C_DESC + E]
        qcol = cst[:, C_Q:C_Q + 1]
        upto = c16[:, 0:P]
        ones16 = c16[:, P:2 * P]

        s_cst, s_ids, s_se = sem("constants_loaded"), sem("ids_loaded"), sem("subjects_gathered")
        s_par = sem("parameters_loaded")
        s_x = [sem(f"x_loaded{i}") for i in range(2)]
        s_w = [sem(f"weights_staged{i}") for i in range(NSTAGE)]
        s_b2 = sem("b2_loaded")
        s_init = sem("out_initialised")
        s_zero = sem("zeros_ready")
        s_spare = sem("spare_rows_written")
        s_vz = sem("vector_rows_cleared")
        s_small_pe, s_small_v, s_small_a = sem("style_products"), sem("style_vector_steps"), sem("style_scalar_steps")
        s_lnv, s_sd = sem("token_stats"), sem("token_deviation")
        s_nrm = sem("token_norm_ready")
        s_xn = sem("x_normalised")
        s_tr = sem("x_transposed")
        s_hT = sem("h_affine_done")
        s_tst, s_tsd, s_h2 = sem("time_stats"), sem("time_deviation"), sem("h_modulated")
        s_back, s_log = sem("h_rows_transposed"), sem("logits_done")
        s_hrow, s_hst = sem("h_rows_copied"), [sem(f"h_rows_stored{i}") for i in range(2)]
        s_lgc = sem("logits_copied")
        s_v = sem("vector_chain")
        s_d, s_exp = sem("logits_less_max"), sem("router_exp")
        s_sel, s_cnt, s_ds, s_dp = sem("selection_ready"), sem("counts_done"), sem("selection_steps_ready"), sem("prefix_done")
        s_comb, s_combst = sem("combine_ready"), sem("combine_stored")
        s_whi, s_wlo = sem("w_hi_ready"), [sem(f"w_lo_ready{i}") for i in range(NSTAGE)]
        s_et = sem("tile_experts_ready")
        s_step, s_tab, s_tok = sem("slot_steps_ready"), sem("slot_table_done"), sem("slot_tokens_ready")
        s_gh = [sem(f"rows_gathered{i}") for i in range(2)]
        s_gt, s_hi, s_lo = sem("tile_transposed"), sem("tile_hi_ready"), sem("tile_lo_ready")
        s_hm, s_relu, s_split = sem("hidden_products"), sem("hidden_relu"), sem("hidden_split")
        s_ym, s_ys, s_yo = sem("y_products"), sem("y_biased"), sem("y_gated")
        s_gate, s_idx, s_sc = sem("gates_ready"), sem("scatter_index_ready"), sem("y_scattered")
        s_held = [sem("gather_waits_carried"), sem("scatter_waits_carried")]
        s_dv, s_fin = sem("vector_tile_chain"), sem("finished")

        def experts(engine, t):
            return nc.values_load_multi_w_load_instructions(
                epairs[0:1].rearrange("p k n -> p (k n)")[:, bass.ds(2 * t, 4)], engines=[engine.engine], min_val=0, max_val=E - 1,
                skip_runtime_bounds_check_because="counts of 1 to E started experts, less 1")[1]

        block = ctx.enter_context(nc.Block())

        @block.sync
        def _(sp_):
            sp_.dma_start(idcol[:, :], ids.rearrange("(b a) -> b a", a=1)).then_inc(s_ids, 16)
            sp_.dma_start(cst[:, :], consts).then_inc(s_cst, 16)
            sp_.dma_start(c16[:, :], consts16).then_inc(s_cst, 16)

            sp_.wait_ge(s_vz, 1)
            sp_.dma_start(vrows[0:64, :], exp_b1.rearrange("e (c p) -> (e c) p", p=P)).then_inc(s_par, 16)
            for at, v in ((V_LNG, ln_g), (V_LNB, ln_b), (V_HB1, hyp_b1), (V_HB2, hyp_b2), (V_SB2, sty_b2)):
                sp_.dma_start(vrows[at:at + v.shape[0] // P, :], v.rearrange("(r p) -> r p", p=P)).then_inc(s_par, 16)
            sp_.dma_start(vrows[V_SB1:V_SB1 + 1, 0:SH // 2], sty_b1.rearrange("(r p) -> r p", r=1)).then_inc(s_par, 16)
            sp_.dma_start(hw1[:, :], hyp_w1).then_inc(s_par, 16)
            sp_.dma_start(hw2[:, :], hyp_w2).then_inc(s_par, 16)
            sp_.dma_start(sw1[:, :], sty_w1).then_inc(s_par, 16)
            sp_.dma_start(sw2[:, :], sty_w2).then_inc(s_par, 16)
            sp_.dma_start(rw[:, :].rearrange("p (k e) -> p k e", k=KD), router_w.rearrange("(k p) e -> p k e", p=P)).then_inc(s_par, 16)

            def load_weights(g, slot):
                if not (isinstance(g, int) and g == 0):
                    sp_.wait_ge(s_wlo[slot], g)
                src = w_v(NSTAGE * g + slot)
                sp_.dma_start(stage[:, slot, :].rearrange("p (a n) -> p a n", a=src.shape[1]), src).then_inc(s_w[slot], 16)

            for slot in range(NSTAGE):
                load_weights(0, slot)
            for u in range(NSTAGE, UNITS):
                load_weights(u // NSTAGE, u % NSTAGE)
            sp_.wait_ge(s_comb, 1)
            for b in range(B):
                sp_.dma_start(comb_v[b], oh1[:, b * JB * E:(b + 1) * JB * E].rearrange("p (j e) -> p j e", e=E)).then_inc(s_combst, 16)
            for par in range(2):
                sp_.wait_ge(s_hst[par], 16 * (B // 2))
            sp_.dma_start(b2row[:, :], exp_b2.rearrange("e d -> (e d)").partition_broadcast(P)).then_inc(s_b2, 16)

        @block.gpsimd
        def _(gp):
            for b in range(2):
                gp.dma_start(xs[:, b, :], x_v[b]).then_inc(s_x[b], 16)
            gp.memset(vrows[:, :], 0.0).then_inc(s_vz, 1)
            gp.memset(zero[:, :], 0.0).then_inc(s_zero, 1)
            gp.wait_ge(s_ids, 16)
            gp.indirect_dma_start(out=se[:, :], out_offset=None, in_=subj_emb,
                                  in_offset=bass.IndirectOffsetOnAxis(ap=idcol[:, 0:1], axis=0)).then_inc(s_se, 16)
            gp.wait_ge(s_zero, 1)
            gp.dma_start(h_dram[N:N + P, :], zero[:, :]).then_inc(s_spare, 16)
            gp.dma_start(h_dram[N + P:ROWS, :], zero[0:8, :]).then_inc(s_spare, 16)
            gp.dma_start(out[N:N + P, :], zero[:, 0:D]).then_inc(s_spare, 16)
            gp.dma_start(out[N + P:ROWS, :], zero[0:8, 0:D]).then_inc(s_spare, 16)

            def start_out(b, par):
                if isinstance(b, int):
                    gp.wait_ge(s_x[par], b // 2 * 16 + 16)
                else:
                    gp.wait_ge(s_x[par], (b - par) * 8 + 16)
                gp.dma_start(out_v[bass.ds(b, 1)].rearrange("b p n -> (b p) n"), xs[:, par, :]).then_inc(s_init, 16)

            with gp.Fori(1, B // 2) as g:
                for par in range(2):
                    b = g * 2 + par
                    start_out(b - 2, par)
                    gp.wait_ge(s_xn, b - 1)
                    gp.wait_ge(s_init, b * 16 - 16)
                    gp.dma_start(xs[:, par, :], x_v[bass.ds(b, 1)].rearrange("b p n -> (b p) n")).then_inc(s_x[par], 16)
            start_out(B - 2, 0)
            start_out(B - 1, 1)

            def carry(t, kind):
                if not (isinstance(t, int) and t == 0):
                    gp.wait_ge(s_held[kind], t)
                gp.tensor_tensor(held_gp[:, kind:kind + 1], zero[0:1, 0:1], zero[0:1, 0:1], ALU.add).then_inc(s_held[kind], 1)

            def gather(t, par):
                gp.wait_ge(s_tok, t + 1)
                if not (isinstance(t, int) and t < 2):
                    gp.wait_ge(s_gate, t - 1)
                carry(t, 0)
                gp.indirect_dma_start(out=hg[:, par, :], out_offset=None, in_=h_dram,
                                      in_offset=bass.IndirectOffsetOnAxis(ap=idxg[par][:, 0:1], axis=0)).then_inc(s_gh[par], 16)

            def scatter(t, par):
                if not (isinstance(t, int) and t == 0):
                    gp.wait_ge(s_sc, t * 16)
                gp.tensor_copy(idxs[par][:, :], tok[:, bass.ds(t, 1)]).then_inc(s_idx, 1)
                gp.wait_ge(s_idx, t + 1)
                gp.wait_ge(s_yo, t + 1)
                carry(t, 1)
                gp.indirect_dma_start(out=out, out_offset=bass.IndirectOffsetOnAxis(ap=idxs[par][:, 0:1], axis=0),
                                      in_=yout[:, par, :], in_offset=None, compute_op=ALU.add).then_inc(s_sc, 16)

            gp.wait_ge(s_hst[0], 16 * (B // 2))
            gp.wait_ge(s_hst[1], 16 * (B // 2))
            gp.wait_ge(s_spare, 16 * 4)
            gp.wait_ge(s_combst, 16 * B)
            gp.wait_ge(s_init, 16 * B)
            for t in range(5):
                gather(t, t % 2)
            for t in range(2, 4):
                scatter(t - 2, t % 2)
                gather(t + 3, 1 - t % 2)
            with gp.Fori(4, TILES - 5, 2) as i:
                for par in range(2):
                    scatter(i + par - 2, par)
                    gather(i + par + 3, 1 - par)
            for t in range(TILES - 5, TILES + 2):
                scatter(t - 2, (t - 2) % 2)
                if t + 3 < TILES:
                    gather(t + 3, (t + 3) % 2)
            gp.wait_ge(s_sc, 16 * TILES)

        @block.scalar
        def _(act):
            def style_softplus():
                act.wait_ge(s_small_v, 10)
                nc.scalar.activation(sp[:, 2, :], sp[:, 1, :], ACT.Exp).then_inc(s_small_a, 1)
                act.wait_ge(s_small_v, 11)
                nc.scalar.activation(sp[:, 4, :], sp[:, 3, :], ACT.Ln).then_inc(s_small_a, 1)

            def deviation(b, par):
                act.wait_ge(s_lnv, b + 1)
                nc.scalar.activation(lnv[:, par, 1, :], lnv[:, par, 0, :], ACT.Sqrt).then_inc(s_sd, 1)

            def normalise(b, par):
                act.wait_ge(s_nrm, b + 1)
                if not (isinstance(b, int) and b < 2):
                    act.wait_ge(s_tr, b - 1)
                for j in range(JB):
                    ins = nc.scalar.activation(xn[:, par, j * D:(j + 1) * D], xs[:, par, j * D:(j + 1) * D], ACT.Identity,
                                               bias=lnv[:, par, 3, j:j + 1], scale=lnv[:, par, 2, j:j + 1])
                ins.then_inc(s_xn, 1)

            def affine(b, par):
                act.wait_ge(s_tr, b + 1)
                if not (isinstance(b, int) and b < 2):
                    act.wait_ge(s_log, b - 1)
                for k in range(KD):
                    ins = nc.scalar.activation(hT[:, par, k * T:(k + 1) * T], bk_T[k][:, :], ACT.Identity,
                                               bias=vcol[:, V_LNB + k:V_LNB + k + 1], scale=vcol[:, V_LNG + k:V_LNG + k + 1])
                ins.then_inc(s_hT, 1)

            def time_deviation(b, par):
                act.wait_ge(s_tst, b + 1)
                nc.scalar.activation(tnv[:, par, 1, :], tnv[:, par, 0, :], ACT.Sqrt).then_inc(s_tsd, 1)

            def rows(b, par):
                act.wait_ge(s_back, b + 1)
                if not (isinstance(b, int) and b < 2):
                    act.wait_ge(s_hst[par], (b - par) * 8)
                for g in range(2):
                    ins = nc.scalar.activation(hrow[:, par, g * 512:(g + 1) * 512], bk_back[g][:, :], ACT.Copy)
                ins.then_inc(s_hrow, 1)
                act.wait_ge(s_hrow, b + 1)
                act.dma_start(h_v[bass.ds(b, 1)].rearrange("b p j d -> (b p) j d"), hrow[:, par, :].rearrange("p (j d) -> p j d", j=JB)).then_inc(s_hst[par], 16)

            def w_hi(g, slot):
                act.wait_ge(s_w[slot], 16 * g + 16)
                nc.scalar.activation(whi[:, bass.ds(g * (NSTAGE * UNIT) + slot * UNIT, UNIT)], stage[:, slot, :],
                                     ACT.Copy, scale=WSCALE).then_inc(s_whi, 1)

            deviation(0, 0)
            normalise(0, 0)
            deviation(1, 1)
            act.wait_ge(s_small_v, 1)
            affine(0, 0)
            normalise(1, 1)
            time_deviation(0, 0)
            for slot in range(NSTAGE):
                w_hi(0, slot)
            style_softplus()
            with act.Fori(1, B // 2) as g:
                for par in range(2):
                    b = g * 2 + par
                    deviation(b, par)
                    affine(b - 1, 1 - par)
                    normalise(b, par)
                    time_deviation(b - 1, 1 - par)
                    rows(b - 2, par)
                    for slot in (2 * par, 2 * par + 1):
                        w_hi(g, slot)
            affine(B - 1, 1)
            time_deviation(B - 1, 1)
            rows(B - 2, 0)
            rows(B - 1, 1)
            act.wait_ge(s_d, 1)
            nc.scalar.activation(ex[:, :], d1[:, :], ACT.Exp).then_inc(s_exp, 1)

            def relu(t, half, b1_t):
                act.wait_ge(s_hm, 2 * t + half + 1)
                for c in range(4 * half, 4 * half + 4):
                    ins = nc.scalar.activation(hid32[:, c * P:(c + 1) * P], bk_hid[half][:, (c - 4 * half) * P:(c - 4 * half + 1) * P],
                                               ACT.Relu, bias=vcol[:, bass.ds(b1_t * FC + c, 1)], scale=1.0 / WSCALE)
                ins.then_inc(s_relu, 1)

            def tile_hi(t, par):
                act.wait_ge(s_gt, t + 1)
                nc.scalar.activation(hThi[:, par, :], bk_g[:, 0:D], ACT.Copy).then_inc(s_hi, 1)

            def gate_y(t, par):
                act.wait_ge(s_ys, t + 1)
                if not (isinstance(t, int) and t < 2):
                    act.wait_ge(s_sc, t * 16 - 16)
                nc.scalar.activation(yout[:, par, :], ysum[:, par, :], ACT.Copy, scale=gates[:, bass.ds(t, 1)]).then_inc(s_yo, 1)

            act.wait_ge(s_et, 1)

            def step(t, par, e):
                relu(t, 0, e)
                if not (isinstance(t, int) and t + 1 == TILES):
                    tile_hi(t + 1, 1 - par)
                if not (isinstance(t, int) and t < 2):
                    gate_y(t - 2, par)
                relu(t, 1, e)

            tile_hi(0, 0)
            es = experts(act, 2)
            for t in range(4):
                step(t, t % 2, es[t])
            with act.Fori(4, TILES - 1, 2) as i:
                es = experts(act, i)
                for par in range(2):
                    step(i + par, par, es[2 + par])
            step(TILES - 1, 0, experts(act, TILES - 1)[2])
            for t in range(TILES, TILES + 2):
                gate_y(t - 2, t % 2)

        @block.tensor
        def _(pe):
            pe.wait_ge(s_cst, 32)

            def transposes(b, par):
                pe.wait_ge(s_xn, b + 1)
                if not (isinstance(b, int) and b == 0):
                    pe.wait_ge(s_hT, b)
                for k in range(KD):
                    for j in range(JB):
                        ins = nc.tensor.transpose(bk_T[k][:, j * P:(j + 1) * P], xn[:, par, j * D + k * P:j * D + (k + 1) * P], ident)
                ins.then_inc(s_tr, 1)

            def back(b, par):
                pe.wait_ge(s_h2, b + 1)
                if not (isinstance(b, int) and b == 0):
                    pe.wait_ge(s_hrow, b)
                for j in range(JB):
                    for k in range(KD):
                        at = (j % 2) * D + k * P
                        ins = nc.tensor.transpose(bk_back[j // 2][:, at:at + P], hT[:, par, k * T + j * P:k * T + (j + 1) * P], ident)
                ins.then_inc(s_back, 1)
                if not (isinstance(b, int) and b < 2):
                    pe.wait_ge(s_lgc, b - 1)
                for j in range(JB):
                    for k in range(KD):
                        ins = nc.tensor.matmul(bk_log[par][:, j * E:(j + 1) * E], hT[:, par, k * T + j * P:k * T + (j + 1) * P],
                                               rw[:, k * E:(k + 1) * E], start=(k == 0), stop=(k == KD - 1))
                ins.then_inc(s_log, 1)

            transposes(0, 0)
            pe.wait_ge(s_par, 16 * 12)
            nc.tensor.transpose(bk_small[:, 0:VEC_ROWS], vrows[0:VEC_ROWS, :], ident[0:VEC_ROWS, 0:VEC_ROWS]).then_inc(s_small_pe, 1)
            transposes(1, 1)
            pe.wait_ge(s_se, 16)
            nc.tensor.transpose(bk_cnt[0:SE, 0:B], se[:, :], ident[0:B, 0:B]).then_inc(s_small_pe, 1)
            pe.wait_ge(s_small_v, 2)
            nc.tensor.matmul(bk_small[:, 0:B], hw1[:, :], sT[0:SE, 0, :], start=True, stop=True).then_inc(s_small_pe, 1)
            pe.wait_ge(s_small_v, 3)
            nc.tensor.matmul(bk_cnt[:, 0:B], hw2[:, :], sT[:, 1, :], start=True, stop=True).then_inc(s_small_pe, 1)
            pe.wait_ge(s_small_v, 4)
            nc.tensor.matmul(bk_small[0:SH // 2, 0:B], sw1[:, :], sT[:, 2, :], start=True, stop=True).then_inc(s_small_pe, 1)
            pe.wait_ge(s_small_v, 5)
            for c in range(4):
                ins = nc.tensor.matmul(bk_cnt[:, c * B:(c + 1) * B], sw2[:, c * P:(c + 1) * P], sT[0:SH // 2, 3, :], start=True, stop=True)
            ins.then_inc(s_small_pe, 1)
            back(0, 0)
            transposes(2, 0)
            back(1, 1)
            with pe.Fori(3, B - 1, 2) as i:
                transposes(i, 1)
                back(i - 1, 0)
                transposes(i + 1, 0)
                back(i, 1)
            transposes(B - 1, 1)
            back(B - 2, 0)
            back(B - 1, 1)

            pe.wait_ge(s_sel, 1)
            nc.tensor.matmul(bk_cnt[:, 0:NBLK], ones16, selh[:, 1:NBLK + 1], start=True, stop=True).then_inc(s_cnt, 1)
            pe.wait_ge(s_ds, 1)
            for h in range(NH):
                ins = nc.tensor.matmul(bk_small[:, h * P:(h + 1) * P], dsel[:, h * P:(h + 1) * P], upto, start=True, stop=True)
            ins.then_inc(s_dp, 1)

            def slot_table(t, par):
                if isinstance(t, int) and t < 3:
                    pe.wait_ge(s_step, t + 1)
                    if t > 0:
                        pe.wait_ge(s_tok, t)
                for h in range(NH):
                    ins = nc.tensor.matmul(bk_tab[:, 0:P + 2], step16[:, par, h, :], table[:, h, :], start=(h == 0), stop=(h == NH - 1))
                ins.then_inc(s_tab, 1)

            def tile_transpose(t, par):
                if isinstance(t, int):
                    pe.wait_ge(s_gh[par], 16 * (t // 2 + 1))
                else:
                    pe.wait_ge(s_gh[par], (t - par) * 8 + 16)
                for k in range(KD):
                    ins = nc.tensor.transpose(bk_g[:, k * P:(k + 1) * P], hg[:, par, k * P:(k + 1) * P], ident)
                ins.then_inc(s_gt, 1)

            def products(half, t, par, e, ty, par_y, e_y):
                yhalf = 1 - half
                if t is not None and half == 0:
                    pe.wait_ge(s_lo, t + 1)
                if t is None or not (isinstance(t, int) and t == 0):
                    pe.wait_ge(s_split, 2 * t + half - 1 if t is not None else 2 * ty + yhalf + 1)
                for i in range(4):
                    if t is not None:
                        c = 4 * half + i
                        o = bk_hid[half][:, i * P:(i + 1) * P]
                        n = 0
                        for w, parts in ((whi, (hThi, hTlo)), (wlo, (hThi,))):
                            for k in range(KD):
                                lhs = w[:, bass.ds(e * (2 * UNIT) + k * FF + c * P, P)]
                                for h in parts:
                                    hid_ins = nc.tensor.matmul(o, lhs, h[:, par, k * P:(k + 1) * P], start=(n == 0), stop=(n == 3 * KD - 1))
                                    n += 1
                    if ty is not None:
                        c = 4 * yhalf + i
                        n = 3 * c
                        for h, ws in ((hidhi, (whi, wlo)), (hidlo, (whi,))):
                            for w in ws:
                                y_ins = nc.tensor.matmul(bk_y[par_y][:, 0:D], h[:, par_y, c * P:(c + 1) * P],
                                                         w[:, bass.ds(e_y * (2 * UNIT) + UNIT + c * D, D)],
                                                         start=(n == 0), stop=(n == 3 * FC - 1))
                                n += 1
                if t is not None:
                    hid_ins.then_inc(s_hm, 1)
                if ty is not None:
                    y_ins.then_inc(s_ym, 1)

            for t in range(3):
                slot_table(t, t % 2)
            pe.wait_ge(s_et, 1)
            pe.wait_ge(s_whi, UNITS)
            for slot in range(NSTAGE):
                pe.wait_ge(s_wlo[slot], len(range(slot, UNITS, NSTAGE)))

            def step(t, par, es):
                def tile(u):
                    return None if isinstance(u, int) and not 0 <= u < TILES else u

                products(0, tile(t), par, es[2], tile(t - 2), par, es[0])
                if tile(t + 1) is not None:
                    tile_transpose(t + 1, 1 - par)
                if tile(t + 3) is not None:
                    slot_table(t + 3, 1 - par)
                products(1, tile(t), par, es[2], tile(t - 1), 1 - par, es[1])

            tile_transpose(0, 0)
            es = experts(pe, 2)
            step(0, 0, [None, None, es[0]])
            step(1, 1, [None, es[0], es[1]])
            step(2, 0, es[0:3])
            step(3, 1, es[1:4])
            with pe.Fori(4, TILES - 3, 2) as i:
                es = experts(pe, i)
                for par in range(2):
                    step(i + par, par, es[par:par + 3])
            for t in range(TILES - 3, TILES, 2):
                es = experts(pe, t)
                for par in range(2):
                    step(t + par, par, es[par:par + 3])
            products(0, None, 0, None, TILES - 1, 0, es[2])

        @block.vector
        def _(ve):
            links = [0]

            def link(ins):
                links[0] += 1
                ins.then_inc(s_v, 1)
                ve.wait_ge(s_v, links[0])

            V = nc.vector
            link(V.memset(selh[:, 0:1], 0.0))
            link(V.memset(start[:, 0:1], 0.0))
            gam_v = gam[:, :].rearrange("p (k b) -> p b k", k=KD)
            bet_v = bet[:, :].rearrange("p (k b) -> p b k", k=KD)

            s_vb = s_dv

            def token_stats(b, par, at):
                if isinstance(b, int):
                    ve.wait_ge(s_x[par], b // 2 * 16 + 16)
                else:
                    ve.wait_ge(s_x[par], (b - par) * 8 + 16)
                for j in range(JB):
                    ins = V.bn_stats(bns[:, j, :], xs[:, par, j * D:(j + 1) * D])
                ins.then_inc(s_vb, 1)
                ve.wait_ge(s_vb, at + 1)
                ve.memset(held_ve[:, :], 0.0)
                for j in range(JB):
                    ins = V.bn_aggr(mv[:, par, j, :], bns[:, j, :])
                ins.then_inc(s_vb, 1)
                ve.wait_ge(s_vb, at + 2)
                V.tensor_scalar(lnv[:, par, 0, :], mv[:, par, :, 1], LN_EPS, None, ALU.add).then_inc(s_lnv, 1)

            def token_norm(b, par, at):
                ve.wait_ge(s_sd, b + 1)
                V.reciprocal(lnv[:, par, 2, :], lnv[:, par, 1, :]).then_inc(s_vb, 1)
                ve.wait_ge(s_vb, at + 1)
                V.scalar_tensor_tensor(out=lnv[:, par, 3, :], in0=mv[:, par, :, 0], scalar=-1.0, in1=lnv[:, par, 2, :],
                                       op0=ALU.mult, op1=ALU.mult).then_inc(s_nrm, 1)

            def time_stats(b, par, at):
                ve.wait_ge(s_hT, b + 1)
                for k in range(KD):
                    ins = V.bn_stats(tns[:, k, :], hT[:, par, k * T:(k + 1) * T])
                ins.then_inc(s_vb, 1)
                ve.wait_ge(s_vb, at + 1)
                ve.memset(held_ve[:, :], 0.0)
                for k in range(KD):
                    ins = V.bn_aggr(tmv[:, par, k, :], tns[:, k, :])
                ins.then_inc(s_vb, 1)
                ve.wait_ge(s_vb, at + 2)
                V.tensor_scalar(tnv[:, par, 0, :], tmv[:, par, :, 1], T_EPS, None, ALU.add).then_inc(s_tst, 1)

            def modulate(b, par, at):
                ve.wait_ge(s_tsd, b + 1)
                V.reciprocal(tnv[:, par, 2, :], tnv[:, par, 1, :]).then_inc(s_vb, 1)
                ve.wait_ge(s_vb, at + 1)
                g_b = gam_v[:, bass.ds(b, 1), :].rearrange("p b k -> p (b k)")
                e_b = bet_v[:, bass.ds(b, 1), :].rearrange("p b k -> p (b k)")
                V.tensor_tensor(tnv[:, par, 3, :], tnv[:, par, 2, :], g_b, ALU.mult).then_inc(s_vb, 1)
                ve.wait_ge(s_vb, at + 2)
                V.tensor_tensor(tnv[:, par, 4, :], tmv[:, par, :, 0], tnv[:, par, 3, :], ALU.mult).then_inc(s_vb, 1)
                ve.wait_ge(s_vb, at + 3)
                V.tensor_tensor(tnv[:, par, 5, :], e_b, tnv[:, par, 4, :], ALU.subtract).then_inc(s_vb, 1)
                ve.wait_ge(s_vb, at + 4)
                for k in range(KD):
                    ins = V.tensor_scalar(hT[:, par, k * T:(k + 1) * T], hT[:, par, k * T:(k + 1) * T],
                                          tnv[:, par, 3, k:k + 1], tnv[:, par, 5, k:k + 1], ALU.mult, ALU.add)
                ins.then_inc(s_h2, 1)

            def copy_logits(b, par):
                ve.wait_ge(s_log, b + 1)
                V.tensor_copy(lg[:, bass.ds(b * JB * E, JB * E)], bk_log[par][:, 0:JB * E]).then_inc(s_lgc, 1)

            L = 9
            token_stats(0, 0, 0)
            token_norm(0, 0, 2)
            token_stats(1, 1, 3)
            ve.wait_ge(s_small_pe, 1)
            V.tensor_copy(vcol[:, :], bk_small[:, 0:VEC_ROWS]).then_inc(s_small_v, 1)
            token_norm(1, 1, 5)
            time_stats(0, 0, 6)
            ve.wait_ge(s_small_pe, 2)
            V.tensor_copy(sT[0:SE, 0, :], bk_cnt[0:SE, 0:B]).then_inc(s_small_v, 1)
            ve.wait_ge(s_small_v, 2)
            ve.wait_ge(s_small_pe, 3)
            V.tensor_scalar(sT[:, 1, :], bk_small[:, 0:B], vcol[:, V_HB1:V_HB1 + 1], 0.0, ALU.add, ALU.max).then_inc(s_small_v, 1)
            ve.wait_ge(s_small_pe, 4)
            V.tensor_scalar(sT[:, 2, :], bk_cnt[:, 0:B], vcol[:, V_HB2:V_HB2 + 1], None, ALU.add).then_inc(s_small_v, 1)
            ve.wait_ge(s_small_pe, 5)
            V.tensor_scalar(sT[0:SH // 2, 3, :], bk_small[0:SH // 2, 0:B], vcol[0:SH // 2, V_SB1:V_SB1 + 1], 0.0, ALU.add, ALU.max).then_inc(s_small_v, 1)
            ve.wait_ge(s_small_pe, 6)
            for c in range(4):
                dst = (gam, bet)[c // 2][:, (c % 2) * B:(c % 2 + 1) * B]
                V.tensor_scalar(dst, bk_cnt[:, c * B:(c + 1) * B], vcol[:, V_SB2 + c:V_SB2 + c + 1], None, ALU.add).then_inc(s_small_v, 1)
            ve.wait_ge(s_small_v, 9)
            link(V.scalar_tensor_tensor(out=sp[:, 0, :], in0=gam[:, :], scalar=-1.0, in1=gam[:, :], op0=ALU.mult, op1=ALU.min))
            V.tensor_scalar(sp[:, 1, :], sp[:, 0, :], 0.0, None, ALU.min).then_inc(s_small_v, 1)
            ve.wait_ge(s_small_a, 1)
            V.tensor_scalar(sp[:, 3, :], sp[:, 2, :], 1.0, None, ALU.add).then_inc(s_small_v, 1)
            ve.wait_ge(s_small_v, 11)
            link(V.tensor_scalar(sp[:, 0, :], sp[:, 3, :], -1.0, None, ALU.add))
            link(V.tensor_scalar(sp[:, 1, :], sp[:, 0, :], 0.0, None, ALU.is_equal))
            link(V.tensor_scalar(sp[:, 5, :], sp[:, 0, :], 1e-30, None, ALU.max))
            ve.wait_ge(s_small_a, 2)
            link(V.reciprocal(sp[:, 3, :], sp[:, 5, :]))
            link(V.tensor_tensor(sp[:, 5, :], sp[:, 4, :], sp[:, 3, :], ALU.mult))
            link(V.tensor_tensor(sp[:, 0, :], sp[:, 5, :], sp[:, 1, :], ALU.add))
            link(V.tensor_tensor(sp[:, 3, :], sp[:, 0, :], sp[:, 2, :], ALU.mult))
            link(V.scalar_tensor_tensor(out=sp[:, 5, :], in0=gam[:, :], scalar=0.0, in1=sp[:, 3, :], op0=ALU.max, op1=ALU.add))
            link(V.tensor_scalar(gam[:, :], sp[:, 5, :], T_EPS, None, ALU.add))

            def w_lo(g, slot):
                at = g * (NSTAGE * UNIT) + slot * UNIT
                ve.wait_ge(s_whi, g * NSTAGE + slot + 1)
                V.scalar_tensor_tensor(out=wlo[:, bass.ds(at, UNIT)], in0=stage[:, slot, :], scalar=WSCALE,
                                       in1=whi[:, bass.ds(at, UNIT)], op0=ALU.mult, op1=ALU.subtract).then_inc(s_wlo[slot], 1)

            def batch(b, par, at):
                token_stats(b, par, at)
                modulate(b - 2, par, at + 2)
                token_norm(b, par, at + 6)
                time_stats(b - 1, 1 - par, at + 7)

            w_lo(0, 0)
            w_lo(0, 1)
            with ve.Fori(1, B // 2) as g:
                for par in range(2):
                    b = g * 2 + par
                    batch(b, par, g * (2 * L) + (par - 2) * L + 8)
                    for slot in (2, 3) if par == 0 else (0, 1):
                        w_lo(g - 1 + par, slot)
                    copy_logits(b - 2, par)
            at = (B - 2) * L + 8
            modulate(B - 2, 0, at)
            time_stats(B - 1, 1, at + 4)
            w_lo(B // 2 - 1, 2)
            modulate(B - 1, 1, at + 6)
            copy_logits(B - 2, 0)
            w_lo(B // 2 - 1, 3)
            copy_logits(B - 1, 1)
            vb_end = at + 10

            def by_expert(a):
                return a.rearrange("p (j e) -> p j e", e=E)

            def over(a):
                return a.unsqueeze(2).broadcast_to([P, NJ, E])

            desc_b = desc.unsqueeze(1).broadcast_to([P, NJ, E])
            lg3, d13, d23, ex3, oh13, tm3 = (by_expert(a[:, :]) for a in (lg, d1, d2, ex, oh1, tm))
            ve.wait_ge(s_lgc, B)
            ve.wait_ge(s_init, 16 * B)
            link(V.memset(ones[:, :], 1.0))
            link(V.tensor_reduce(m8[:, 0, :], lg3, AX_X, ALU.max))
            V.tensor_tensor(d13, lg3, over(m8[:, 0, :]), ALU.subtract).then_inc(s_d, 1)
            ve.wait_ge(s_d, 1)
            link(V.scalar_tensor_tensor(out=tm3, in0=d13, scalar=0.0, in1=desc_b, op0=ALU.is_ge, op1=ALU.mult))
            link(V.tensor_reduce(m8[:, 1, :], tm3, AX_X, ALU.max))
            link(V.tensor_tensor(oh13, desc_b, over(m8[:, 1, :]), ALU.is_equal))
            link(V.scalar_tensor_tensor(out=d2[:, :], in0=oh1[:, :], scalar=-3e38, in1=d1[:, :], op0=ALU.mult, op1=ALU.add))
            link(V.tensor_reduce(m8[:, 2, :], d23, AX_X, ALU.max))
            link(V.tensor_tensor(tm3, d23, over(m8[:, 2, :]), ALU.is_ge))
            link(V.tensor_tensor(d23, tm3, desc_b, ALU.mult))
            link(V.tensor_reduce(m8[:, 3, :], d23, AX_X, ALU.max))
            link(V.tensor_tensor(tm3, desc_b, over(m8[:, 3, :]), ALU.is_equal))
            link(V.tensor_tensor(d2[:, :], tm[:, :], oh1[:, :], ALU.add))
            V.tensor_copy(selh[:, 1:NBLK + 1].rearrange("p (e j) -> p j e", e=E), d23).then_inc(s_sel, 1)
            ve.wait_ge(s_sel, 1)
            V.tensor_tensor(dsel[:, :], selh[:, 1:NBLK + 1], selh[:, 0:NBLK], ALU.subtract).then_inc(s_ds, 1)

            ve.wait_ge(s_exp, 1)
            link(V.tensor_reduce(m8[:, 4, :], ex3, AX_X, ALU.add))
            link(V.reciprocal(m8[:, 5, :], m8[:, 4, :]))
            link(V.tensor_tensor(ex3, ex3, over(m8[:, 5, :]), ALU.mult))
            link(V.tensor_tensor(tm[:, :], ex[:, :], d2[:, :], ALU.mult))
            link(V.tensor_reduce(m8[:, 6, :], tm3, AX_X, ALU.add))
            link(V.reciprocal(m8[:, 7, :], m8[:, 6, :]))
            V.tensor_tensor(oh13, tm3, over(m8[:, 7, :]), ALU.mult).then_inc(s_comb, 1)

            ve.wait_ge(s_cnt, 1)
            cnt = bk_cnt[:, 0:NBLK]
            link(V.tensor_tensor_scan(csum[:, :], ones[:, :], cnt, 0.0, ALU.mult, ALU.add))
            link(V.tensor_reduce(ne[:, 0, :], cnt.rearrange("p (e j) -> p e j", e=E), AX_X, ALU.add))
            link(V.tensor_scalar(nei[:, 0, :], ne[:, 0, :], float(P - 1), None, ALU.add))
            link(V.tensor_single_scalar(nei[:, 1, :], nei[:, 0, :], -P, ALU.bitwise_and))
            link(V.tensor_copy(ne[:, 1, :], nei[:, 1, :]))
            link(V.tensor_tensor_scan(ne[:, 2, :], ones[:, 0:E], ne[:, 1, :], 0.0, ALU.mult, ALU.add))
            link(V.tensor_tensor(ne[:, 3, :], ne[:, 2, :], ne[:, 1, :], ALU.subtract))
            link(V.tensor_tensor(ne[:, 4, :], csum[:, :].rearrange("p (e j) -> p e j", e=E)[:, :, NJ - 1], ne[:, 0, :], ALU.subtract))
            link(V.tensor_tensor(ne[:, 5, :], ne[:, 3, :], ne[:, 4, :], ALU.subtract))
            link(V.tensor_tensor(dstart[:, :], csum[:, :], cnt, ALU.subtract))
            link(V.tensor_tensor(start[:, 1:NBLK + 1].rearrange("p (e j) -> p e j", e=E), dstart[:, :].rearrange("p (e j) -> p e j", e=E),
                                 ne[:, 5, :].unsqueeze(2).broadcast_to([P, E, NJ]), ALU.add))
            link(V.tensor_tensor(dstart[:, :], start[:, 1:NBLK + 1], start[:, 0:NBLK], ALU.subtract))
            for h in range(NH):
                V.tensor_tensor_reduce(tm[:, 0:P], start[:, 1 + h * P:1 + (h + 1) * P], ident, 1.0, 0.0, ALU.mult, ALU.add,
                                       stcol[:, h:h + 1])
                ins = V.tensor_tensor_reduce(tm[:, P:2 * P], dstart[:, h * P:(h + 1) * P], ident, 1.0, 0.0, ALU.mult, ALU.add,
                                             stcol[:, NH + h:NH + h + 1])
                link(ins)
            ve.wait_ge(s_dp, 1)
            for h in range(NH):
                V.tensor_scalar(table[:, h, 0:P], bk_small[:, h * P:(h + 1) * P], stcol[:, NH + h:NH + h + 1], None, ALU.add)
                link(V.tensor_copy(table[:, h, P:P + 2], cst[:, C_DJ + 2 * h:C_DJ + 2 * h + 2]))

            t128 = cst[:, C_T128:C_T128 + 72].unsqueeze(2).broadcast_to([P, 72, E])
            ge3 = ge[:, :].rearrange("p (t e) -> p t e", e=E)
            link(V.tensor_tensor(ge3, t128, ne[:, 3, :].unsqueeze(1).broadcast_to([P, 72, E]), ALU.is_ge))
            link(V.tensor_reduce(tm[:, 0:72], ge3, AX_X, ALU.add))
            link(V.tensor_scalar(etile[:, :], tm[:, 0:72], -1.0, None, ALU.add))
            link(V.memset(epairs[:, 0, :], 0))
            pairs = etile[:, :].rearrange("p (k n) -> p k n", n=2)
            V.tensor_copy(epairs[:, 1:36, 0:2], pairs[:, 0:35, :])
            V.tensor_copy(epairs[:, :, 2:4], pairs).then_inc(s_et, 1)

            def slot_steps(t, par):
                for h in range(NH):
                    ins = V.tensor_scalar(step16[:, par, h, :], slotrow, stcol[:, h:h + 1], cst[:, bass.ds(t + C_NEGT, 1)],
                                          ALU.subtract, ALU.is_ge)
                ins.then_inc(s_step, 1)

            def tokens_compare(t, par):
                ve.wait_ge(s_tab, t + 1)
                V.tensor_scalar(junk, bk_tab[:, 0:P], cst[:, bass.ds(t + C_SLOTCOL, 1)], None, ALU.is_le).then_inc(s_dv, 1)
                V.tensor_tensor_reduce(rj[:, :], bk_tab[:, P:P + 2], cst[:, C_TOK2:C_TOK2 + 2], 1.0, 0.0,
                                       ALU.mult, ALU.add, rt[:, par, 1:2]).then_inc(s_dv, 1)

            def tokens_count(par, done):
                ve.wait_ge(s_dv, done)
                V.tensor_reduce(rt[:, par, 0:1], junk, AX_X, ALU.add).then_inc(s_dv, 1)

            def tokens_place(par, done):
                ve.wait_ge(s_dv, done)
                V.tensor_scalar(rt[:, par, 2:3], rt[:, par, 0:1], float(P), qcol, ALU.is_ge, ALU.mult)
                V.scalar_tensor_tensor(out=rt[:, par, 3:4], in0=rt[:, par, 0:1], scalar=float(JB), in1=rt[:, par, 1:2],
                                       op0=ALU.mult, op1=ALU.add).then_inc(s_dv, 1)

            def tokens_index(t, par, done):
                if isinstance(t, int) and t == 2:
                    ve.wait_ge(s_gh[par], 16)
                ve.wait_ge(s_dv, done)
                V.tensor_tensor(idxg[par][:, :], rt[:, par, 2:3], rt[:, par, 3:4], ALU.add)
                V.tensor_tensor(tok[:, bass.ds(t, 1)], rt[:, par, 2:3], rt[:, par, 3:4], ALU.add).then_inc(s_tok, 1)

            def gate(t, par, e):
                V.tensor_copy(gates[:, bass.ds(t, 1)], hg[:, par, bass.ds(e + D, 1)]).then_inc(s_gate, 1)

            def tile_lo(t, par):
                ve.wait_ge(s_hi, t + 1)
                V.tensor_tensor(hTlo[:, par, :], bk_g[:, 0:D], hThi[:, par, :], ALU.subtract).then_inc(s_lo, 1)

            def split_hi(t, par, half):
                ve.wait_ge(s_relu, 2 * t + half + 1)
                a, b = half * 512, half * 512 + 512
                V.tensor_copy(hidhi[:, par, a:b], hid32[:, a:b]).then_inc(s_dv, 1)

            def split_lo(par, half, done):
                a, b = half * 512, half * 512 + 512
                ve.wait_ge(s_dv, done)
                V.tensor_tensor(hidlo[:, par, a:b], hid32[:, a:b], hidhi[:, par, a:b], ALU.subtract).then_inc(s_split, 1)

            def bias_y(t, par, e):
                ve.wait_ge(s_ym, 2 * t + 2)
                V.scalar_tensor_tensor(out=ysum[:, par, :], in0=bk_y[par][:, 0:D], scalar=1.0 / WSCALE,
                                       in1=b2row[:, bass.ds(e * D, D)], op0=ALU.mult, op1=ALU.add).then_inc(s_ys, 1)

            at = vb_end
            slot_steps(0, 0)
            slot_steps(1, 1)
            for t in range(3):
                tokens_compare(t, t % 2)
                tokens_count(t % 2, at + 2)
                tokens_place(t % 2, at + 3)
                tokens_index(t, t % 2, at + 4)
                at += 4
                if t < 2:
                    slot_steps(t + 2, t % 2)
            tile_lo(0, 0)
            ve.wait_ge(s_b2, 16)

            def step(t, par, at, e, e_y):
                def tile(u):
                    return not isinstance(u, int) or 0 <= u < TILES

                other, tokens = 1 - par, tile(t + 3)
                gate(t, par, e)
                if tile(t - 2):
                    bias_y(t - 2, par, e_y)
                if tile(t + 4):
                    slot_steps(t + 4, par)
                split_hi(t, par, 0)
                if tokens:
                    tokens_compare(t + 3, other)
                split_lo(par, 0, at + 1)
                if tile(t + 1):
                    tile_lo(t + 1, other)
                n = 1
                if tokens:
                    tokens_count(other, at + 3)
                    n = 4
                split_hi(t, par, 1)
                if tokens:
                    tokens_place(other, at + 4)
                split_lo(par, 1, at + n + 1)
                if tokens:
                    tokens_index(t + 3, other, at + 6)
                return 6 if tokens else 2

            base = at
            es = experts(ve, 2)
            LT = step(0, 0, base, es[0], None)
            for t in range(1, 4):
                step(t, t % 2, t * LT + base, es[t], es[t - 2])
            with ve.Fori(4, TILES - 5, 2) as i:
                es = experts(ve, i)
                for par in range(2):
                    step(i + par, par, (i + par) * LT + base, es[2 + par], es[par])
            at = (TILES - 5) * LT + base
            for t in range(TILES - 5, TILES, 2):
                es = experts(ve, t)
                for par in range(2):
                    if t + par < TILES:
                        at += step(t + par, par, at, es[2 + par], es[par])
            bias_y(TILES - 2, 1, es[1])
            bias_y(TILES - 1, 0, es[2])


def constants():
    import numpy as np

    c = np.zeros((P, C_END), np.float32)
    q = np.arange(P)
    c[:, C_ID:C_ID + P] = np.eye(P)
    c[:, C_SLOT:C_SLOT + P] = q
    t = np.arange(72)
    c[:, C_NEGT:C_NEGT + 72] = -P * t
    c[:, C_SLOTCOL:C_SLOTCOL + 72] = P * t + q[:, None]
    c[:, C_Q] = q
    pair = np.arange(NBLK)
    for i, v in enumerate((pair % NJ // JB, pair % JB)):
        step = np.diff(v, prepend=0)
        for h in range(NH):
            c[:, C_DJ + 2 * h + i] = step[h * P:(h + 1) * P]
    c[:, C_DESC:C_DESC + E] = E - np.arange(E)
    c[:, C_TOK2] = T
    c[:, C_TOK2 + 1] = 1
    c[:, C_T128:C_T128 + 72] = P * t
    c16 = np.ones((P, 2 * P), np.float16)
    c16[:, 0:P] = q[:, None] <= q
    return c, c16


_INS = ["x", "itok_B_6_14"] + ["L0_cond_" + n for n in (
    "ln_g", "ln_b", "subj_emb", "hyp_w1", "hyp_b1", "hyp_w2", "hyp_b2", "sty_w1", "sty_b1", "sty_w2", "sty_b2",
    "router_w", "exp_w1", "exp_b1", "exp_w2", "exp_b2")]


def kernel(**inputs):
    import numpy as np
    import concourse.bacc as bacc
    from concourse.bass_utils import run_bass_kernel_spmd

    nc = bacc.Bacc("TRN2", target_bir_lowering=False, num_devices=1)
    arrays, args = {}, []
    named = [(n, np.ascontiguousarray(inputs[n])) for n in _INS] + list(zip(("consts", "consts16"), constants()))
    for name, a in named:
        arrays[f"in_{name}"] = a
        args.append(nc.dram_tensor(f"in_{name}", a.shape, mybir.dt.from_np(a.dtype), kind="ExternalInput").ap())
    args.append(nc.dram_tensor("out_rows", (ROWS, D), F32, kind="ExternalOutput").ap())
    moe_kernel(nc, *args)
    r = run_bass_kernel_spmd(nc, [arrays], core_ids=[0])
    return r.results[0]["out_rows"][:N].reshape(B, T, D)
```

```python
from contextlib import ExitStack

import concourse.bass as bass
from concourse import mybir

F32 = mybir.dt.float32
F16 = mybir.dt.float16
I32 = mybir.dt.int32
ALU = mybir.AluOpType
ACT = mybir.ActivationFunctionType
AX_X = mybir.AxisListType.X

P = 128
B, T, D = 8, 512, 256
E, FF = 8, 1024
NSUBJ, SE, SH = 32, 64, 128
N = B * T
KD = D // P
FC = FF // P
JB = T // P
NJ = N // P
PARTS = ((0, (B - 2) * JB), ((B - 2) * JB, NJ))
NBLK = E * NJ
NH = NBLK // P
TILES = (2 * N + E * (P - 1)) // P
ROWS = N + P + 8
HROW = D + E
WSCALE = 64.0
LN_EPS, T_EPS = 1e-5, 1e-8
UNIT = 2 * FF
UNITS = 2 * E
NSTAGE = 4
VEC_ROWS = 75
V_LNG, V_LNB, V_HB1, V_HB2, V_SB1, V_SB2 = 64, 66, 68, 69, 70, 71

C_ID, C_SLOT, C_NEGT, C_SLOTCOL, C_Q, C_DJ, C_DESC, C_TOK2, C_T128 = 0, 128, 256, 328, 400, 401, 405, 413, 415
C_END = C_T128 + 72


def moe_kernel(nc, x, ids, ln_g, ln_b, subj_emb, hyp_w1, hyp_b1, hyp_w2, hyp_b2, sty_w1, sty_b1,
               sty_w2, sty_b2, router_w, exp_w1, exp_b1, exp_w2, exp_b2, consts, consts16, out):
    h_dram = nc.dram_tensor("h_rows", (ROWS, HROW), F32).ap()
    x_v = x.rearrange("b (p j) d -> b p (j d)", j=JB)
    out_v = out[0:N, :].rearrange("(b p j) d -> b p (j d)", b=B, j=JB)
    h_v = h_dram[0:N, 0:D].rearrange("(b p j) d -> b p j d", b=B, j=JB)
    comb_v = h_dram[0:N, D:HROW].rearrange("(b p j) e -> b p j e", b=B, j=JB)
    w1_v = exp_w1.rearrange("e (k p) f -> e p k f", p=P)
    w2_v = exp_w2.rearrange("e (c p) d -> e p c d", p=P)

    def w_v(u):
        return (w2_v if u % 2 else w1_v)[u // 2]

    with ExitStack() as ctx:
        def sb(name, shape, dt=F32):
            return ctx.enter_context(nc.sbuf_tensor(name, shape, dt))

        def sem(name):
            return ctx.enter_context(nc.semaphore(name))

        whi = sb("whi", [P, UNITS * UNIT], F16)
        wlo = sb("wlo", [P, UNITS * UNIT], F16)
        stage = sb("stage", [P, NSTAGE, UNIT])
        cst = sb("cst", [P, C_END])
        c16 = sb("c16", [P, 2 * P], F16)

        xs = sb("xs", [P, 2, JB * D])
        xn = sb("xn", [P, 2, JB * D])
        hT = sb("hT", [P, 2, KD * T])
        hrow = sb("hrow", [P, 2, JB * D])
        hid32 = stage[:, 0, 0:FF]
        hidhi = stage[:, 1, 0:FF].bitcast(F16).rearrange("p (a f) -> p a f", a=2)
        hidlo = stage[:, 2, 0:FF].bitcast(F16).rearrange("p (a f) -> p a f", a=2)
        b2row = hrow[:, :, :].rearrange("p a n -> p (a n)")
        hg = xs[:, 0, 0:2 * HROW].rearrange("p (a d) -> p a d", a=2)
        ysum = xn[:, 0, 2 * D:4 * D].rearrange("p (a d) -> p a d", a=2)
        yout = xs[:, 1, 0:2 * D].rearrange("p (a d) -> p a d", a=2)
        hThi = xn[:, 0, 0:D].bitcast(F16).rearrange("p (a d) -> p a d", a=2)
        hTlo = xn[:, 0, D:2 * D].bitcast(F16).rearrange("p (a d) -> p a d", a=2)
        step16 = xn[:, 1, 0:2 * P].bitcast(F16).rearrange("p (a h s) -> p a h s", a=2, h=NH)
        junk = xn[:, 1, 2 * P:3 * P]

        hw1 = hrow[0:SE, 1, 0:SH]
        hw2 = hrow[:, 1, SH:2 * SH]
        sw1 = hrow[:, 1, 2 * SH:2 * SH + SH // 2]
        sw2 = hrow[0:SH // 2, 1, 320:320 + 2 * D]
        d1, d2, ex, oh1 = (xs[:, 0, i * NBLK:(i + 1) * NBLK] for i in range(4))
        tm = xn[:, 1, 3 * P:5 * P]
        sums = xn[:, 1, 5 * P:7 * P]
        csum, dstart = xn[:, 0, 2 * D:3 * D], xn[:, 0, 3 * D:4 * D]
        ones = xn[:, 0, 0:NBLK]
        ge = xs[:, 1, 0:72 * E]

        vrows = sb("vrows", [P, P])
        vcol = sb("vcol", [P, VEC_ROWS])
        rw = sb("rw", [P, KD * E])
        idcol = sb("idcol", [B, 1], I32)
        se = sb("se", [B, SE])
        sT = sb("sT", [P, 4, B])
        gam = sb("gam", [P, KD * B])
        bet = sb("bet", [P, KD * B])
        sp = sb("sp", [P, 6, KD * B])
        bns = sb("bns", [P, JB, 6])
        mv = sb("mv", [P, 2, JB, 2])
        lnv = sb("lnv", [P, 2, 4, JB])
        tns = sb("tns", [P, KD, 6])
        tmv = sb("tmv", [P, 2, KD, 2])
        tnv = sb("tnv", [P, 2, 6, KD])
        lg = sb("lg", [P, NJ * E])
        selh = sb("selh", [P, NBLK + 1], F16)
        dsel = sb("dsel", [P, NBLK], F16)
        m8 = sb("m8", [P, 8, NJ])
        start = sb("start", [P, NBLK + 1])
        ne = sb("ne", [P, 6, E])
        nei = sb("nei", [P, 2, E], I32)
        stcol = sb("stcol", [P, 2 * NH])
        table = sb("table", [P, NH, P + 2], F16)
        etile = sb("etile", [P, 2 + 72 + 8], I32)
        tok = sb("tok", [P, 72], I32)
        gates = sb("gates", [P, 72])
        rt = sb("rt", [P, 2, 4])
        rj = sb("rj", [P, 2])
        idxg = [sb(f"idxg{i}", [P, 1], I32) for i in range(2)]
        idxs = [sb(f"idxs{i}", [P, 1], I32) for i in range(2)]
        zero = sb("zero", [P, HROW])
        held_gp = sb("held_gp", [1, 3])
        held_ve = sb("held_ve", [1, 1])

        banks = [ctx.enter_context(nc.psum_tensor(f"bank{i}", [P, 512], F32)) for i in range(8)]
        bk_T = banks[0:2]
        bk_back = banks[2:4]
        bk_log = banks[4:6]
        bk_small = banks[6]
        bk_cnt = banks[7]
        bk_hid = banks[0:2]
        bk_y = banks[2:4]
        bk_g = banks[4]
        bk_tab = banks[5]

        ident = cst[:, C_ID:C_ID + P]
        slotrow = cst[:, C_SLOT:C_SLOT + P]
        desc = cst[:, C_DESC:C_DESC + E]
        qcol = cst[:, C_Q:C_Q + 1]
        upto = c16[:, 0:P]
        ones16 = c16[:, P:2 * P]

        s_cst, s_ids, s_se = sem("constants_loaded"), sem("ids_loaded"), sem("subjects_gathered")
        s_cst16, s_par = sem("constants16_loaded"), sem("parameters_loaded")
        s_x = [sem(f"x_loaded{i}") for i in range(2)]
        s_w = [sem(f"weights_staged{i}") for i in range(NSTAGE)]
        s_b2 = sem("b2_loaded")
        s_init = [sem(f"out_initialised{i}") for i in range(2)]
        s_zero = sem("zeros_ready")
        s_spare = sem("spare_rows_written")
        s_vz = sem("vector_rows_cleared")
        s_small_pe, s_small_v, s_small_a = sem("style_products"), sem("style_vector_steps"), sem("style_scalar_steps")
        s_lnv, s_sd = sem("token_stats"), sem("token_deviation")
        s_nrm = sem("token_norm_ready")
        s_xn = sem("x_normalised")
        s_tr = sem("x_transposed")
        s_hT = sem("h_affine_done")
        s_tst, s_tsd, s_mc, s_h2 = sem("time_stats"), sem("time_deviation"), sem("modulation_ready"), sem("h_modulated")
        s_back, s_log = sem("h_rows_transposed"), sem("logits_done")
        s_hrow, s_hst = sem("h_rows_copied"), [sem(f"h_rows_stored{i}") for i in range(2)]
        s_lgc = sem("logits_copied")
        s_v = sem("vector_chain")
        s_gp, s_sum, s_rec = sem("combine_chain"), sem("combine_sums_ready"), sem("combine_reciprocals_ready")
        s_d, s_exp = sem("logits_less_max"), sem("router_exp")
        s_sel, s_cnt, s_ds, s_dp = sem("selection_ready"), sem("counts_done"), sem("selection_steps_ready"), sem("prefix_done")
        s_comb, s_combst = sem("combine_ready"), sem("combine_stored")
        s_whi, s_wlo = sem("w_hi_ready"), [sem(f"w_lo_ready{i}") for i in range(NSTAGE)]
        s_wsc, s_wlast = sem("last_weights_scaled"), sem("last_w_lo_ready")
        s_et = sem("tile_experts_ready")
        s_step, s_tab, s_tok = sem("slot_steps_ready"), sem("slot_table_done"), sem("slot_tokens_ready")
        s_gh = [sem(f"rows_gathered{i}") for i in range(2)]
        s_gt, s_hi, s_lo = sem("tile_transposed"), sem("tile_hi_ready"), sem("tile_lo_ready")
        s_hm, s_relu, s_split = sem("hidden_products"), sem("hidden_relu"), sem("hidden_split")
        s_ym, s_ys, s_yo = sem("y_products"), sem("y_biased"), sem("y_gated")
        s_gate, s_idx, s_sc = sem("gates_ready"), sem("scatter_index_ready"), sem("y_scattered")
        s_held = [sem("gather_waits_carried"), sem("scatter_waits_carried"), sem("modulation_waits_carried")]
        s_dv = sem("vector_tile_chain")

        def experts(engine, t, n=4):
            return nc.values_load_multi_w_load_instructions(
                etile[0:1, bass.ds(t, n + 2)], engines=[engine.engine], min_val=0, max_val=E - 1,
                skip_runtime_bounds_check_because="counts of 1 to E started experts, less 1")[1]

        whi_bytes, wlo_bytes = (w[:, :].bitcast(mybir.dt.uint8) for w in (whi, wlo))

        def weights(w_bytes, e, at, n):
            return w_bytes[:, bass.ds(e * (4 * UNIT) + 2 * at, 2 * n)].bitcast(F16)

        block = ctx.enter_context(nc.Block())

        @block.sync
        def _(sp_):
            sp_.dma_start(idcol[:, :], ids.rearrange("(b a) -> b a", a=1)).then_inc(s_ids, 16)
            sp_.dma_start(cst[:, :], consts).then_inc(s_cst, 16)

            sp_.wait_ge(s_vz, 1)
            sp_.dma_start(vrows[0:64, :], exp_b1.rearrange("e (c p) -> (e c) p", p=P)).then_inc(s_par, 16)
            for at, v in ((V_LNG, ln_g), (V_LNB, ln_b), (V_HB1, hyp_b1), (V_HB2, hyp_b2), (V_SB2, sty_b2)):
                sp_.dma_start(vrows[at:at + v.shape[0] // P, :], v.rearrange("(r p) -> r p", p=P)).then_inc(s_par, 16)
            sp_.dma_start(vrows[V_SB1:V_SB1 + 1, 0:SH // 2], sty_b1.rearrange("(r p) -> r p", r=1)).then_inc(s_par, 16)
            sp_.dma_start(hw1[:, :], hyp_w1).then_inc(s_par, 16)
            sp_.dma_start(hw2[:, :], hyp_w2).then_inc(s_par, 16)
            sp_.dma_start(sw1[:, :], sty_w1).then_inc(s_par, 16)
            sp_.dma_start(sw2[:, :], sty_w2).then_inc(s_par, 16)
            sp_.dma_start(rw[:, :].rearrange("p (k e) -> p k e", k=KD), router_w.rearrange("(k p) e -> p k e", p=P)).then_inc(s_par, 16)
            sp_.dma_start(c16[:, :], consts16).then_inc(s_cst16, 16)

            def load_weights(g, slot):
                if not (isinstance(g, int) and g == 0):
                    sp_.wait_ge(s_wlo[slot], g)
                src = w_v(NSTAGE * g + slot)
                sp_.dma_start(stage[:, slot, :].rearrange("p (a n) -> p a n", a=src.shape[1]), src).then_inc(s_w[slot], 16)

            for slot in range(NSTAGE):
                load_weights(0, slot)
            load_weights(1, 0)
            load_weights(1, 1)

            def store_h(b, par):
                sp_.wait_ge(s_hrow, b + 1)
                sp_.dma_start(h_v[bass.ds(b, 1)].rearrange("b p j d -> (b p) j d"),
                              hrow[:, par, :].rearrange("p (j d) -> p j d", j=JB)).then_inc(s_hst[par], 16)

            with sp_.Fori(1, B // 2 - 1) as g:
                load_weights(g, 2)
                load_weights(g, 3)
                store_h(g * 2 - 2, 0)
                load_weights(g + 1, 0)
                load_weights(g + 1, 1)
                store_h(g * 2 - 1, 1)
            load_weights(B // 2 - 1, 2)
            load_weights(B // 2 - 1, 3)
            for b in range(B - 4, B - 1):
                store_h(b, b % 2)
            for part, batches in enumerate((range(0, B - 2), range(B - 2, B))):
                if part == 1:
                    store_h(B - 1, 1)
                sp_.wait_ge(s_comb, part + 1)
                for b in batches:
                    sp_.dma_start(comb_v[b], oh1[:, b * JB * E:(b + 1) * JB * E].rearrange("p (j e) -> p j e", e=E)).then_inc(s_combst, 16)
            for par in range(2):
                sp_.wait_ge(s_hst[par], 16 * (B // 2))
            sp_.dma_start(b2row[:, :], exp_b2.rearrange("e d -> (e d)").partition_broadcast(P)).then_inc(s_b2, 16)

        @block.gpsimd
        def _(gp):
            gp.memset(vrows[:, :], 0.0).then_inc(s_vz, 1)
            for b in range(2):
                gp.dma_start(xs[:, b, :], x_v[b]).then_inc(s_x[b], 16)
            gp.memset(zero[:, :], 0.0).then_inc(s_zero, 1)
            gp.wait_ge(s_ids, 16)
            gp.indirect_dma_start(out=se[:, :], out_offset=None, in_=subj_emb,
                                  in_offset=bass.IndirectOffsetOnAxis(ap=idcol[:, 0:1], axis=0)).then_inc(s_se, 16)
            gp.wait_ge(s_zero, 1)
            gp.dma_start(h_dram[N:N + P, :], zero[:, :]).then_inc(s_spare, 16)
            gp.dma_start(h_dram[N + P:ROWS, :], zero[0:8, :]).then_inc(s_spare, 16)
            gp.dma_start(out[N:N + P, :], zero[:, 0:D]).then_inc(s_spare, 16)
            gp.dma_start(out[N + P:ROWS, :], zero[0:8, 0:D]).then_inc(s_spare, 16)

            def carry(t, kind):
                if not (isinstance(t, int) and t == 0):
                    gp.wait_ge(s_held[kind], t)
                gp.tensor_tensor(held_gp[:, kind:kind + 1], zero[0:1, 0:1], zero[0:1, 0:1], ALU.add).then_inc(s_held[kind], 1)

            def start_out(b, par):
                if isinstance(b, int):
                    gp.wait_ge(s_x[par], b // 2 * 16 + 16)
                else:
                    gp.wait_ge(s_x[par], (b - par) * 8 + 16)
                gp.dma_start(out_v[bass.ds(b, 1)].rearrange("b p n -> (b p) n"), xs[:, par, :]).then_inc(s_init[par], 16)

            def load_x(b, par):
                gp.wait_ge(s_xn, b - 1)
                gp.wait_ge(s_init[par], (b - par) * 8)
                gp.dma_start(xs[:, par, :], x_v[bass.ds(b, 1)].rearrange("b p n -> (b p) n")).then_inc(s_x[par], 16)

            def modulate(b, par):
                gp.wait_ge(s_mc, b + 1)
                carry(b, 2)
                for k in range(KD):
                    ins = gp.tensor_scalar(hT[:, par, k * T:(k + 1) * T], hT[:, par, k * T:(k + 1) * T],
                                           tnv[:, par, 3, k:k + 1], tnv[:, par, 5, k:k + 1], ALU.mult, ALU.add)
                ins.then_inc(s_h2, 1)

            for b in range(2):
                start_out(b, b)
                load_x(b + 2, b)
            with gp.Fori(1, B // 2 - 1) as g:
                for par in range(2):
                    b = g * 2 + par
                    modulate(b - 2, par)
                    start_out(b, par)
                    load_x(b + 2, par)
            for b in range(B - 2, B):
                modulate(b - 2, b % 2)
                start_out(b, b % 2)
            modulate(B - 2, 0)
            modulate(B - 1, 1)
            held = [0]

            def link(ins):
                held[0] += 1
                ins.then_inc(s_gp, 1)
                gp.wait_ge(s_gp, held[0])

            def combine(part, j0, j1):
                n = j1 - j0

                def over(i):
                    return m8[:, i, j0:j1].unsqueeze(2).broadcast_to([P, n, E])

                ex3, chosen3, oh13, half_sums = (a[:, j0 * E:j1 * E].rearrange("p (j e) -> p j e", e=E) for a in (ex, d2, oh1, sums))
                def total(out, v3):
                    half, quarter = half_sums[:, :, 0:4], half_sums[:, :, 4:6]
                    link(gp.tensor_tensor(half, v3[:, :, 0:4], v3[:, :, 4:8], ALU.add))
                    link(gp.tensor_tensor(quarter, half[:, :, 0:2], half[:, :, 2:4], ALU.add))
                    gp.tensor_tensor(out.unsqueeze(2), quarter[:, :, 0:1], quarter[:, :, 1:2], ALU.add).then_inc(s_sum, 1)

                gp.wait_ge(s_exp, part + 1)
                total(m8[:, 4, j0:j1], ex3)
                gp.wait_ge(s_rec, 2 * part + 1)
                link(gp.tensor_tensor(ex3, ex3, over(5), ALU.mult))
                gp.wait_ge(s_sel, part + 1)
                link(gp.tensor_tensor(ex3, ex3, chosen3, ALU.mult))
                total(m8[:, 6, j0:j1], ex3)
                gp.wait_ge(s_rec, 2 * part + 2)
                gp.tensor_tensor(oh13, ex3, over(7), ALU.mult).then_inc(s_comb, 1)

            def last_w_lo(i):
                u = UNITS - 2 + i
                gp.wait_ge(s_wsc, i + 1)
                gp.tensor_tensor(wlo[:, u * UNIT:(u + 1) * UNIT], stage[:, u % NSTAGE, :], whi[:, u * UNIT:(u + 1) * UNIT],
                                 ALU.subtract).then_inc(s_wlast, 1)

            for part in range(2):
                combine(part, *PARTS[part])
            last_w_lo(0)

            def gather(t, par):
                gp.wait_ge(s_tok, t + 1)
                if not (isinstance(t, int) and t < 2):
                    gp.wait_ge(s_gate, t - 1)
                carry(t, 0)
                gp.indirect_dma_start(out=hg[:, par, :], out_offset=None, in_=h_dram,
                                      in_offset=bass.IndirectOffsetOnAxis(ap=idxg[par][:, 0:1], axis=0)).then_inc(s_gh[par], 16)

            def scatter(t, par):
                if not (isinstance(t, int) and t == 0):
                    gp.wait_ge(s_sc, t * 16)
                gp.tensor_copy(idxs[par][:, :], tok[:, bass.ds(t, 1)]).then_inc(s_idx, 1)
                gp.wait_ge(s_idx, t + 1)
                gp.wait_ge(s_yo, t + 1)
                carry(t, 1)
                gp.indirect_dma_start(out=out, out_offset=bass.IndirectOffsetOnAxis(ap=idxs[par][:, 0:1], axis=0),
                                      in_=yout[:, par, :], in_offset=None, compute_op=ALU.add).then_inc(s_sc, 16)

            gp.wait_ge(s_hst[0], 16 * (B // 2))
            gp.wait_ge(s_hst[1], 16 * (B // 2))
            gp.wait_ge(s_spare, 16 * 4)
            gp.wait_ge(s_combst, 16 * B)
            gp.wait_ge(s_init[0], 16 * (B // 2))
            gp.wait_ge(s_init[1], 16 * (B // 2))
            for t in range(5):
                if t == 2:
                    last_w_lo(1)
                gather(t, t % 2)
            for t in range(2, 4):
                scatter(t - 2, t % 2)
                gather(t + 3, 1 - t % 2)
            with gp.Fori(4, TILES - 5, 2) as i:
                for par in range(2):
                    scatter(i + par - 2, par)
                    gather(i + par + 3, 1 - par)
            for t in range(TILES - 5, TILES + 2):
                scatter(t - 2, (t - 2) % 2)
                if t + 3 < TILES:
                    gather(t + 3, (t + 3) % 2)
            gp.wait_ge(s_sc, 16 * TILES)

        @block.scalar
        def _(act):
            def style_softplus():
                act.wait_ge(s_small_v, 10)
                nc.scalar.activation(sp[:, 2, :], sp[:, 1, :], ACT.Exp).then_inc(s_small_a, 1)
                act.wait_ge(s_small_v, 11)
                nc.scalar.activation(sp[:, 4, :], sp[:, 3, :], ACT.Ln).then_inc(s_small_a, 1)

            def deviation(b, par):
                act.wait_ge(s_lnv, b + 1)
                nc.scalar.activation(lnv[:, par, 1, :], lnv[:, par, 0, :], ACT.Sqrt).then_inc(s_sd, 1)

            def normalise(b, par):
                act.wait_ge(s_nrm, b + 1)
                if not (isinstance(b, int) and b < 2):
                    act.wait_ge(s_tr, b - 1)
                for j in range(JB):
                    ins = nc.scalar.activation(xn[:, par, j * D:(j + 1) * D], xs[:, par, j * D:(j + 1) * D], ACT.Identity,
                                               bias=lnv[:, par, 3, j:j + 1], scale=lnv[:, par, 2, j:j + 1])
                ins.then_inc(s_xn, 1)

            def affine(b, par):
                act.wait_ge(s_tr, b + 1)
                if not (isinstance(b, int) and b < 2):
                    act.wait_ge(s_log, b - 1)
                for k in range(KD):
                    ins = nc.scalar.activation(hT[:, par, k * T:(k + 1) * T], bk_T[k][:, :], ACT.Identity,
                                               bias=vcol[:, V_LNB + k:V_LNB + k + 1], scale=vcol[:, V_LNG + k:V_LNG + k + 1])
                ins.then_inc(s_hT, 1)

            def time_deviation(b, par):
                act.wait_ge(s_tst, b + 1)
                nc.scalar.activation(tnv[:, par, 1, :], tnv[:, par, 0, :], ACT.Sqrt).then_inc(s_tsd, 1)

            def rows(b, par):
                act.wait_ge(s_back, b + 1)
                if not (isinstance(b, int) and b < 2):
                    act.wait_ge(s_hst[par], (b - par) * 8)
                for g in range(2):
                    ins = nc.scalar.activation(hrow[:, par, g * 512:(g + 1) * 512], bk_back[g][:, :], ACT.Copy)
                ins.then_inc(s_hrow, 1)

            def w_hi(g, slot):
                act.wait_ge(s_w[slot], 16 * g + 16)
                nc.scalar.activation(whi[:, bass.ds(g * (NSTAGE * UNIT) + slot * UNIT, UNIT)], stage[:, slot, :],
                                     ACT.Copy, scale=WSCALE).then_inc(s_whi, 1)

            deviation(0, 0)
            normalise(0, 0)
            deviation(1, 1)
            act.wait_ge(s_small_v, 1)
            affine(0, 0)
            normalise(1, 1)
            style_softplus()
            w_hi(0, 0)
            w_hi(0, 1)
            with act.Fori(1, B // 2) as g:
                for par in range(2):
                    b = g * 2 + par
                    time_deviation(b - 2, par)
                    affine(b - 1, 1 - par)
                    w_hi(g - 1 + par, 2 - 2 * par)
                    deviation(b, par)
                    normalise(b, par)
                    w_hi(g - 1 + par, 3 - 2 * par)
                    rows(b - 2, par)
            time_deviation(B - 2, 0)
            affine(B - 1, 1)
            time_deviation(B - 1, 1)

            def router_exp(part, j0, j1):
                act.wait_ge(s_d, part + 1)
                nc.scalar.activation(ex[:, j0 * E:j1 * E], d1[:, j0 * E:j1 * E], ACT.Exp).then_inc(s_exp, 1)

            def scale_stage(u):
                at = stage[:, u % NSTAGE, :]
                nc.scalar.activation(at, at, ACT.Copy, scale=WSCALE).then_inc(s_wsc, 1)

            router_exp(0, *PARTS[0])
            w_hi(UNITS // NSTAGE - 1, NSTAGE - 2)
            scale_stage(UNITS - 2)
            router_exp(1, *PARTS[1])
            rows(B - 2, 0)
            w_hi(UNITS // NSTAGE - 1, NSTAGE - 1)
            rows(B - 1, 1)
            scale_stage(UNITS - 1)

            def relu(t, half, b1_t):
                act.wait_ge(s_hm, 2 * t + half + 1)
                for c in range(4 * half, 4 * half + 4):
                    ins = nc.scalar.activation(hid32[:, c * P:(c + 1) * P], bk_hid[half][:, (c - 4 * half) * P:(c - 4 * half + 1) * P],
                                               ACT.Relu, bias=vcol[:, bass.ds(b1_t * FC + c, 1)], scale=1.0 / WSCALE)
                ins.then_inc(s_relu, 1)

            def tile_hi(t, par):
                act.wait_ge(s_gt, t + 1)
                nc.scalar.activation(hThi[:, par, :], bk_g[:, 0:D], ACT.Copy).then_inc(s_hi, 1)

            def gate_y(t, par):
                act.wait_ge(s_ys, t + 1)
                if not (isinstance(t, int) and t < 2):
                    act.wait_ge(s_sc, t * 16 - 16)
                nc.scalar.activation(yout[:, par, :], ysum[:, par, :], ACT.Copy, scale=gates[:, bass.ds(t, 1)]).then_inc(s_yo, 1)

            def step(t, par, e):
                relu(t, 0, e)
                if not (isinstance(t, int) and t + 1 == TILES):
                    tile_hi(t + 1, 1 - par)
                if not (isinstance(t, int) and t < 2):
                    gate_y(t - 2, par)
                relu(t, 1, e)

            tile_hi(0, 0)
            act.wait_ge(s_et, 1)
            es = experts(act, 0)
            for t in range(4):
                step(t, t % 2, es[2 + t])
            with act.Fori(4, TILES - 3, 4) as i:
                es = experts(act, i)
                for q in range(4):
                    step(i + q, q % 2, es[2 + q])
            es = experts(act, TILES - 3)
            for t in range(TILES - 3, TILES):
                step(t, t % 2, es[t - TILES + 5])
            for t in range(TILES, TILES + 2):
                gate_y(t - 2, t % 2)

        @block.tensor
        def _(pe):
            pe.wait_ge(s_cst, 16)

            def transposes(b, par):
                pe.wait_ge(s_xn, b + 1)
                if not (isinstance(b, int) and b == 0):
                    pe.wait_ge(s_hT, b)
                for k in range(KD):
                    for j in range(JB):
                        ins = nc.tensor.transpose(bk_T[k][:, j * P:(j + 1) * P], xn[:, par, j * D + k * P:j * D + (k + 1) * P], ident)
                ins.then_inc(s_tr, 1)

            def back(b, par):
                pe.wait_ge(s_h2, b + 1)
                if not (isinstance(b, int) and b == 0):
                    pe.wait_ge(s_hrow, b)
                for j in range(JB):
                    for k in range(KD):
                        at = (j % 2) * D + k * P
                        ins = nc.tensor.transpose(bk_back[j // 2][:, at:at + P], hT[:, par, k * T + j * P:k * T + (j + 1) * P], ident)
                ins.then_inc(s_back, 1)

            def logits(b, par):
                if not (isinstance(b, int) and b < 2):
                    pe.wait_ge(s_lgc, b - 1)
                for j in range(JB):
                    for k in range(KD):
                        ins = nc.tensor.matmul(bk_log[par][:, j * E:(j + 1) * E], hT[:, par, k * T + j * P:k * T + (j + 1) * P],
                                               rw[:, k * E:(k + 1) * E], start=(k == 0), stop=(k == KD - 1))
                ins.then_inc(s_log, 1)

            transposes(0, 0)
            pe.wait_ge(s_par, 16 * 12)
            nc.tensor.transpose(bk_small[:, 0:VEC_ROWS], vrows[0:VEC_ROWS, :], ident[0:VEC_ROWS, 0:VEC_ROWS]).then_inc(s_small_pe, 1)
            pe.wait_ge(s_se, 16)
            nc.tensor.transpose(bk_cnt[0:SE, 0:B], se[:, :], ident[0:B, 0:B]).then_inc(s_small_pe, 1)
            pe.wait_ge(s_small_v, 2)
            nc.tensor.matmul(bk_small[:, 0:B], hw1[:, :], sT[0:SE, 0, :], start=True, stop=True).then_inc(s_small_pe, 1)
            pe.wait_ge(s_small_v, 3)
            nc.tensor.matmul(bk_cnt[:, 0:B], hw2[:, :], sT[:, 1, :], start=True, stop=True).then_inc(s_small_pe, 1)
            pe.wait_ge(s_small_v, 4)
            nc.tensor.matmul(bk_small[0:SH // 2, 0:B], sw1[:, :], sT[:, 2, :], start=True, stop=True).then_inc(s_small_pe, 1)
            pe.wait_ge(s_small_v, 5)
            for c in range(4):
                ins = nc.tensor.matmul(bk_cnt[:, c * B:(c + 1) * B], sw2[:, c * P:(c + 1) * P], sT[0:SH // 2, 3, :], start=True, stop=True)
            ins.then_inc(s_small_pe, 1)
            transposes(1, 1)
            back(0, 0)
            logits(0, 0)
            transposes(2, 0)
            back(1, 1)
            logits(1, 1)
            with pe.Fori(3, B - 1, 2) as i:
                transposes(i, 1)
                back(i - 1, 0)
                logits(i - 1, 0)
                transposes(i + 1, 0)
                back(i, 1)
                logits(i, 1)
            transposes(B - 1, 1)
            for b in range(B - 2, B):
                pe.wait_ge(s_h2, b + 1)
                logits(b, b % 2)
            for b in range(B - 2, B):
                back(b, b % 2)

            pe.wait_ge(s_cst16, 16)
            pe.wait_ge(s_sel, 2)
            nc.tensor.matmul(bk_cnt[:, 0:NBLK], ones16, selh[:, 1:NBLK + 1], start=True, stop=True).then_inc(s_cnt, 1)
            pe.wait_ge(s_ds, 1)
            for h in range(NH):
                ins = nc.tensor.matmul(bk_small[:, h * P:(h + 1) * P], dsel[:, h * P:(h + 1) * P], upto, start=True, stop=True)
            ins.then_inc(s_dp, 1)

            def slot_table(t, par):
                if isinstance(t, int) and t < 4:
                    pe.wait_ge(s_step, t + 1)
                    if t > 0:
                        pe.wait_ge(s_tok, t)
                for h in range(NH):
                    ins = nc.tensor.matmul(bk_tab[:, 0:P + 2], step16[:, par, h, :], table[:, h, :], start=(h == 0), stop=(h == NH - 1))
                ins.then_inc(s_tab, 1)

            def tile_transpose(t, par):
                if isinstance(t, int):
                    pe.wait_ge(s_gh[par], 16 * (t // 2 + 1))
                else:
                    pe.wait_ge(s_gh[par], (t - par) * 8 + 16)
                for k in range(KD):
                    ins = nc.tensor.transpose(bk_g[:, k * P:(k + 1) * P], hg[:, par, k * P:(k + 1) * P], ident)
                ins.then_inc(s_gt, 1)

            def products(half, t, par, e, ty, par_y, e_y):
                yhalf = 1 - half
                if t is not None and half == 0:
                    pe.wait_ge(s_lo, t + 1)
                if t is None or not (isinstance(t, int) and t == 0):
                    pe.wait_ge(s_split, 2 * t + half - 1 if t is not None else 2 * ty + yhalf + 1)
                for i in range(4):
                    if t is not None:
                        c = 4 * half + i
                        o = bk_hid[half][:, i * P:(i + 1) * P]
                        n = 0
                        for w, parts in ((whi_bytes, (hThi, hTlo)), (wlo_bytes, (hThi,))):
                            for k in range(KD):
                                lhs = weights(w, e, k * FF + c * P, P)
                                for h in parts:
                                    hid_ins = nc.tensor.matmul(o, lhs, h[:, par, k * P:(k + 1) * P], start=(n == 0), stop=(n == 3 * KD - 1))
                                    n += 1
                    if ty is not None:
                        c = 4 * yhalf + i
                        n = 3 * c
                        for h, ws in ((hidhi, (whi_bytes, wlo_bytes)), (hidlo, (whi_bytes,))):
                            for w in ws:
                                y_ins = nc.tensor.matmul(bk_y[par_y][:, 0:D], h[:, par_y, c * P:(c + 1) * P],
                                                         weights(w, e_y, UNIT + c * D, D),
                                                         start=(n == 0), stop=(n == 3 * FC - 1))
                                n += 1
                if t is not None:
                    hid_ins.then_inc(s_hm, 1)
                if ty is not None:
                    y_ins.then_inc(s_ym, 1)

            slot_table(0, 0)
            slot_table(1, 1)
            tile_transpose(0, 0)
            slot_table(2, 0)
            pe.wait_ge(s_whi, UNITS)
            for slot in range(NSTAGE):
                pe.wait_ge(s_wlo[slot], len(range(slot, UNITS - 2, NSTAGE)))
            pe.wait_ge(s_wlast, 1)

            def step(t, par, es):
                def tile(u):
                    return None if isinstance(u, int) and not 0 <= u < TILES else u

                products(0, tile(t), par, es[2], tile(t - 2), par, es[0])
                if tile(t + 1) is not None:
                    tile_transpose(t + 1, 1 - par)
                if tile(t + 3) is not None:
                    slot_table(t + 3, 1 - par)
                products(1, tile(t), par, es[2], tile(t - 1), 1 - par, es[1])

            pe.wait_ge(s_et, 1)
            es = experts(pe, 0)
            for t in range(4):
                if t == 1:
                    pe.wait_ge(s_wlast, 2)
                step(t, t % 2, es[t:t + 3])
            with pe.Fori(4, TILES - 3, 8) as i:
                es = experts(pe, i, 8)
                for q in range(8):
                    step(i + q, q % 2, es[q:q + 3])
            es = experts(pe, TILES - 3)
            for t in range(TILES - 3, TILES + 1):
                step(t, t % 2, es[t - TILES + 3:][:3])
            products(0, None, 0, None, TILES - 1, 0, es[4])

        @block.vector
        def _(ve):
            links = [0]

            def link(ins):
                links[0] += 1
                ins.then_inc(s_v, 1)
                ve.wait_ge(s_v, links[0])

            V = nc.vector
            link(V.memset(selh[:, 0:1], 0.0))
            link(V.memset(start[:, 0:1], 0.0))
            gam_v = gam[:, :].rearrange("p (k b) -> p b k", k=KD)
            bet_v = bet[:, :].rearrange("p (k b) -> p b k", k=KD)

            def token_stats(b, par, at):
                if isinstance(b, int):
                    ve.wait_ge(s_x[par], b // 2 * 16 + 16)
                else:
                    ve.wait_ge(s_x[par], (b - par) * 8 + 16)
                for j in range(JB):
                    ins = V.bn_stats(bns[:, j, :], xs[:, par, j * D:(j + 1) * D])
                ins.then_inc(s_dv, 1)
                ve.wait_ge(s_dv, at + 1)
                ve.memset(held_ve[:, :], 0.0)
                for j in range(JB):
                    ins = V.bn_aggr(mv[:, par, j, :], bns[:, j, :])
                ins.then_inc(s_dv, 1)
                ve.wait_ge(s_dv, at + 2)
                V.tensor_scalar(lnv[:, par, 0, :], mv[:, par, :, 1], LN_EPS, None, ALU.add).then_inc(s_lnv, 1)

            def token_norm(b, par, at):
                ve.wait_ge(s_sd, b + 1)
                V.reciprocal(lnv[:, par, 2, :], lnv[:, par, 1, :]).then_inc(s_dv, 1)
                ve.wait_ge(s_dv, at + 1)
                V.scalar_tensor_tensor(out=lnv[:, par, 3, :], in0=mv[:, par, :, 0], scalar=-1.0, in1=lnv[:, par, 2, :],
                                       op0=ALU.mult, op1=ALU.mult).then_inc(s_nrm, 1)

            def time_stats(b, par, at):
                ve.wait_ge(s_hT, b + 1)
                for k in range(KD):
                    ins = V.bn_stats(tns[:, k, :], hT[:, par, k * T:(k + 1) * T])
                ins.then_inc(s_dv, 1)
                ve.wait_ge(s_dv, at + 1)
                ve.memset(held_ve[:, :], 0.0)
                for k in range(KD):
                    ins = V.bn_aggr(tmv[:, par, k, :], tns[:, k, :])
                ins.then_inc(s_dv, 1)
                ve.wait_ge(s_dv, at + 2)
                V.tensor_scalar(tnv[:, par, 0, :], tmv[:, par, :, 1], T_EPS, None, ALU.add).then_inc(s_tst, 1)

            def modulation(b, par, at):
                ve.wait_ge(s_tsd, b + 1)
                V.reciprocal(tnv[:, par, 2, :], tnv[:, par, 1, :]).then_inc(s_dv, 1)
                ve.wait_ge(s_dv, at + 1)
                g_b = gam_v[:, bass.ds(b, 1), :].rearrange("p b k -> p (b k)")
                e_b = bet_v[:, bass.ds(b, 1), :].rearrange("p b k -> p (b k)")
                V.tensor_tensor(tnv[:, par, 3, :], tnv[:, par, 2, :], g_b, ALU.mult).then_inc(s_dv, 1)
                ve.wait_ge(s_dv, at + 2)
                V.tensor_tensor(tnv[:, par, 4, :], tmv[:, par, :, 0], tnv[:, par, 3, :], ALU.mult).then_inc(s_dv, 1)
                ve.wait_ge(s_dv, at + 3)
                V.tensor_tensor(tnv[:, par, 5, :], e_b, tnv[:, par, 4, :], ALU.subtract).then_inc(s_mc, 1)

            def copy_logits(b, par):
                ve.wait_ge(s_log, b + 1)
                V.tensor_copy(lg[:, bass.ds(b * JB * E, JB * E)], bk_log[par][:, 0:JB * E]).then_inc(s_lgc, 1)

            L = 8
            token_stats(0, 0, 0)
            token_norm(0, 0, 2)
            token_stats(1, 1, 3)
            ve.wait_ge(s_small_pe, 1)
            V.tensor_copy(vcol[:, :], bk_small[:, 0:VEC_ROWS]).then_inc(s_small_v, 1)
            token_norm(1, 1, 5)
            ve.wait_ge(s_small_pe, 2)
            V.tensor_copy(sT[0:SE, 0, :], bk_cnt[0:SE, 0:B]).then_inc(s_small_v, 1)
            ve.wait_ge(s_small_v, 2)
            ve.wait_ge(s_small_pe, 3)
            V.tensor_scalar(sT[:, 1, :], bk_small[:, 0:B], vcol[:, V_HB1:V_HB1 + 1], 0.0, ALU.add, ALU.max).then_inc(s_small_v, 1)
            ve.wait_ge(s_small_pe, 4)
            V.tensor_scalar(sT[:, 2, :], bk_cnt[:, 0:B], vcol[:, V_HB2:V_HB2 + 1], None, ALU.add).then_inc(s_small_v, 1)
            ve.wait_ge(s_small_pe, 5)
            V.tensor_scalar(sT[0:SH // 2, 3, :], bk_small[0:SH // 2, 0:B], vcol[0:SH // 2, V_SB1:V_SB1 + 1], 0.0, ALU.add, ALU.max).then_inc(s_small_v, 1)
            ve.wait_ge(s_small_pe, 6)
            for c in range(4):
                dst = (gam, bet)[c // 2][:, (c % 2) * B:(c % 2 + 1) * B]
                V.tensor_scalar(dst, bk_cnt[:, c * B:(c + 1) * B], vcol[:, V_SB2 + c:V_SB2 + c + 1], None, ALU.add).then_inc(s_small_v, 1)
            ve.wait_ge(s_small_v, 9)
            link(V.scalar_tensor_tensor(out=sp[:, 0, :], in0=gam[:, :], scalar=-1.0, in1=gam[:, :], op0=ALU.mult, op1=ALU.min))
            V.tensor_scalar(sp[:, 1, :], sp[:, 0, :], 0.0, None, ALU.min).then_inc(s_small_v, 1)
            time_stats(0, 0, 6)
            ve.wait_ge(s_small_a, 1)
            V.tensor_scalar(sp[:, 3, :], sp[:, 2, :], 1.0, None, ALU.add).then_inc(s_small_v, 1)
            ve.wait_ge(s_small_v, 11)
            link(V.tensor_scalar(sp[:, 0, :], sp[:, 3, :], -1.0, None, ALU.add))
            link(V.tensor_scalar(sp[:, 1, :], sp[:, 0, :], 0.0, None, ALU.is_equal))
            link(V.tensor_scalar(sp[:, 5, :], sp[:, 0, :], 1e-30, None, ALU.max))
            ve.wait_ge(s_small_a, 2)
            link(V.reciprocal(sp[:, 3, :], sp[:, 5, :]))
            link(V.tensor_tensor(sp[:, 5, :], sp[:, 4, :], sp[:, 3, :], ALU.mult))
            link(V.tensor_tensor(sp[:, 0, :], sp[:, 5, :], sp[:, 1, :], ALU.add))
            link(V.tensor_tensor(sp[:, 3, :], sp[:, 0, :], sp[:, 2, :], ALU.mult))
            link(V.scalar_tensor_tensor(out=sp[:, 5, :], in0=gam[:, :], scalar=0.0, in1=sp[:, 3, :], op0=ALU.max, op1=ALU.add))
            link(V.tensor_scalar(gam[:, :], sp[:, 5, :], T_EPS, None, ALU.add))

            def w_lo(g, slot):
                at = g * (NSTAGE * UNIT) + slot * UNIT
                ve.wait_ge(s_whi, g * NSTAGE + slot + 1)
                V.scalar_tensor_tensor(out=wlo[:, bass.ds(at, UNIT)], in0=stage[:, slot, :], scalar=WSCALE,
                                       in1=whi[:, bass.ds(at, UNIT)], op0=ALU.mult, op1=ALU.subtract).then_inc(s_wlo[slot], 1)

            w_lo(0, 0)
            w_lo(0, 1)
            with ve.Fori(1, B // 2) as g:
                for par in range(2):
                    b = g * 2 + par
                    at = g * (2 * L) + (par - 2) * L + 8
                    first = 2 - 2 * par
                    modulation(b - 2, par, at)
                    token_stats(b, par, at + 3)
                    token_norm(b, par, at + 5)
                    w_lo(g - 1 + par, first)
                    time_stats(b - 1, 1 - par, at + 6)
                    w_lo(g - 1 + par, first + 1)
                    copy_logits(b - 2, par)
            at = (B - 2) * L + 8
            modulation(B - 2, 0, at)
            time_stats(B - 1, 1, at + 3)
            modulation(B - 1, 1, at + 5)
            links_batches = at + 8
            link(V.memset(ones[:, :], 1.0))

            def reciprocals(part, i):
                j0, j1 = PARTS[part]
                ve.wait_ge(s_sum, 2 * part + i + 1)
                V.reciprocal(m8[:, 5 + 2 * i, j0:j1], m8[:, 4 + 2 * i, j0:j1]).then_inc(s_rec, 1)

            def select(part, j0, j1):
                n = j1 - j0
                cols = slice(j0 * E, j1 * E)

                def over(i):
                    return m8[:, i, j0:j1].unsqueeze(2).broadcast_to([P, n, E])

                desc_b = desc.unsqueeze(1).broadcast_to([P, n, E])
                lg_, d1_, d2_, oh1_, tm_ = (a[:, cols] for a in (lg, d1, d2, oh1, tm))
                lg3, d13, d23, oh13, tm3 = (a.rearrange("p (j e) -> p j e", e=E) for a in (lg_, d1_, d2_, oh1_, tm_))
                link(V.tensor_reduce(m8[:, 0, j0:j1], lg3, AX_X, ALU.max))
                V.tensor_tensor(d13, lg3, over(0), ALU.subtract).then_inc(s_d, 1)
                ve.wait_ge(s_d, part + 1)
                link(V.scalar_tensor_tensor(out=tm3, in0=d13, scalar=0.0, in1=desc_b, op0=ALU.is_ge, op1=ALU.mult))
                link(V.tensor_reduce(m8[:, 1, j0:j1], tm3, AX_X, ALU.max))
                link(V.tensor_tensor(oh13, desc_b, over(1), ALU.is_equal))
                if part == 1:
                    reciprocals(0, 1)
                link(V.scalar_tensor_tensor(out=d2_, in0=oh1_, scalar=-3e38, in1=d1_, op0=ALU.mult, op1=ALU.add))
                link(V.tensor_reduce(m8[:, 2, j0:j1], d23, AX_X, ALU.max))
                link(V.tensor_tensor(tm3, d23, over(2), ALU.is_ge))
                link(V.tensor_tensor(d23, tm3, desc_b, ALU.mult))
                link(V.tensor_reduce(m8[:, 3, j0:j1], d23, AX_X, ALU.max))
                if part == 0:
                    reciprocals(0, 0)
                link(V.tensor_tensor(tm3, desc_b, over(3), ALU.is_equal))
                link(V.tensor_tensor(d2_, tm_, oh1_, ALU.add))
                V.tensor_copy(selh[:, 1:NBLK + 1].rearrange("p (e j) -> p j e", e=E)[:, j0:j1, :], d23).then_inc(s_sel, 1)
                if j1 == NJ:
                    ve.wait_ge(s_sel, 2)
                    V.tensor_tensor(dsel[:, :], selh[:, 1:NBLK + 1], selh[:, 0:NBLK], ALU.subtract).then_inc(s_ds, 1)

            ve.wait_ge(s_init[0], 16 * (B // 2))
            ve.wait_ge(s_lgc, B - 2)
            select(0, *PARTS[0])
            copy_logits(B - 2, 0)
            copy_logits(B - 1, 1)
            ve.wait_ge(s_lgc, B)
            ve.wait_ge(s_init[1], 16 * (B // 2))
            select(1, *PARTS[1])

            reciprocals(1, 0)
            ve.wait_ge(s_cnt, 1)
            cnt = bk_cnt[:, 0:NBLK]
            link(V.tensor_tensor_scan(csum[:, :], ones[:, :], cnt, 0.0, ALU.mult, ALU.add))
            link(V.tensor_reduce(ne[:, 0, :], cnt.rearrange("p (e j) -> p e j", e=E), AX_X, ALU.add))
            link(V.tensor_scalar(nei[:, 0, :], ne[:, 0, :], float(P - 1), None, ALU.add))
            link(V.tensor_single_scalar(nei[:, 1, :], nei[:, 0, :], -P, ALU.bitwise_and))
            link(V.tensor_copy(ne[:, 1, :], nei[:, 1, :]))
            link(V.tensor_tensor_scan(ne[:, 2, :], ones[:, 0:E], ne[:, 1, :], 0.0, ALU.mult, ALU.add))
            link(V.tensor_tensor(ne[:, 3, :], ne[:, 2, :], ne[:, 1, :], ALU.subtract))
            link(V.tensor_tensor(ne[:, 4, :], csum[:, :].rearrange("p (e j) -> p e j", e=E)[:, :, NJ - 1], ne[:, 0, :], ALU.subtract))
            link(V.tensor_tensor(ne[:, 5, :], ne[:, 3, :], ne[:, 4, :], ALU.subtract))
            reciprocals(1, 1)
            link(V.tensor_tensor(dstart[:, :], csum[:, :], cnt, ALU.subtract))
            link(V.tensor_tensor(start[:, 1:NBLK + 1].rearrange("p (e j) -> p e j", e=E), dstart[:, :].rearrange("p (e j) -> p e j", e=E),
                                 ne[:, 5, :].unsqueeze(2).broadcast_to([P, E, NJ]), ALU.add))
            link(V.tensor_tensor(dstart[:, :], start[:, 1:NBLK + 1], start[:, 0:NBLK], ALU.subtract))
            for h in range(NH):
                V.tensor_tensor_reduce(tm[:, 0:P], start[:, 1 + h * P:1 + (h + 1) * P], ident, 1.0, 0.0, ALU.mult, ALU.add,
                                       stcol[:, h:h + 1])
                ins = V.tensor_tensor_reduce(tm[:, P:2 * P], dstart[:, h * P:(h + 1) * P], ident, 1.0, 0.0, ALU.mult, ALU.add,
                                             stcol[:, NH + h:NH + h + 1])
                link(ins)
            ve.wait_ge(s_dp, 1)
            for h in range(NH):
                V.tensor_scalar(table[:, h, 0:P], bk_small[:, h * P:(h + 1) * P], stcol[:, NH + h:NH + h + 1], None, ALU.add)
                link(V.tensor_copy(table[:, h, P:P + 2], cst[:, C_DJ + 2 * h:C_DJ + 2 * h + 2]))

            def slot_steps(t, par):
                for h in range(NH):
                    ins = V.tensor_scalar(step16[:, par, h, :], slotrow, stcol[:, h:h + 1], cst[:, bass.ds(t + C_NEGT, 1)],
                                          ALU.subtract, ALU.is_ge)
                ins.then_inc(s_step, 1)

            def tokens_compare(t, par):
                ve.wait_ge(s_tab, t + 1)
                V.tensor_scalar(junk, bk_tab[:, 0:P], cst[:, bass.ds(t + C_SLOTCOL, 1)], None, ALU.is_le).then_inc(s_dv, 1)
                V.tensor_tensor_reduce(rj[:, :], bk_tab[:, P:P + 2], cst[:, C_TOK2:C_TOK2 + 2], 1.0, 0.0,
                                       ALU.mult, ALU.add, rt[:, par, 1:2]).then_inc(s_dv, 1)

            def tokens_count(par, done):
                ve.wait_ge(s_dv, done)
                V.tensor_reduce(rt[:, par, 0:1], junk, AX_X, ALU.add).then_inc(s_dv, 1)

            def tokens_place(par, done):
                ve.wait_ge(s_dv, done)
                V.tensor_scalar(rt[:, par, 2:3], rt[:, par, 0:1], float(P), qcol, ALU.is_ge, ALU.mult)
                V.scalar_tensor_tensor(out=rt[:, par, 3:4], in0=rt[:, par, 0:1], scalar=float(JB), in1=rt[:, par, 1:2],
                                       op0=ALU.mult, op1=ALU.add).then_inc(s_dv, 1)

            def tokens_index(t, par, done):
                if isinstance(t, int) and t == 2:
                    ve.wait_ge(s_gh[par], 16)
                ve.wait_ge(s_dv, done)
                V.tensor_tensor(idxg[par][:, :], rt[:, par, 2:3], rt[:, par, 3:4], ALU.add)
                V.tensor_tensor(tok[:, bass.ds(t, 1)], rt[:, par, 2:3], rt[:, par, 3:4], ALU.add).then_inc(s_tok, 1)

            def gate(t, par, e):
                V.tensor_copy(gates[:, bass.ds(t, 1)], hg[:, par, bass.ds(e + D, 1)]).then_inc(s_gate, 1)

            def tile_lo(t, par):
                ve.wait_ge(s_hi, t + 1)
                V.tensor_tensor(hTlo[:, par, :], bk_g[:, 0:D], hThi[:, par, :], ALU.subtract).then_inc(s_lo, 1)

            def split_hi(t, par, half):
                ve.wait_ge(s_relu, 2 * t + half + 1)
                a, b = half * 512, half * 512 + 512
                V.tensor_copy(hidhi[:, par, a:b], hid32[:, a:b]).then_inc(s_dv, 1)

            def split_lo(par, half, done):
                a, b = half * 512, half * 512 + 512
                ve.wait_ge(s_dv, done)
                V.tensor_tensor(hidlo[:, par, a:b], hid32[:, a:b], hidhi[:, par, a:b], ALU.subtract).then_inc(s_split, 1)

            def bias_y(t, par, e):
                ve.wait_ge(s_ym, 2 * t + 2)
                V.scalar_tensor_tensor(out=ysum[:, par, :], in0=bk_y[par][:, 0:D], scalar=1.0 / WSCALE,
                                       in1=b2row[:, bass.ds(e * D, D)], op0=ALU.mult, op1=ALU.add).then_inc(s_ys, 1)

            def tile_experts():
                t128 = cst[:, C_T128:C_T128 + 72].unsqueeze(2).broadcast_to([P, 72, E])
                ge3 = ge[:, :].rearrange("p (t e) -> p t e", e=E)
                link(V.tensor_tensor(ge3, t128, ne[:, 3, :].unsqueeze(1).broadcast_to([P, 72, E]), ALU.is_ge))
                link(V.tensor_reduce(tm[:, 0:72], ge3, AX_X, ALU.add))
                link(V.memset(etile[:, :], 0))
                V.tensor_scalar(etile[:, 2:74], tm[:, 0:72], -1.0, None, ALU.add).then_inc(s_et, 1)

            at = links_batches
            slot_steps(0, 0)
            slot_steps(1, 1)
            for t in range(3):
                tokens_compare(t, t % 2)
                tokens_count(t % 2, at + 2)
                tokens_place(t % 2, at + 3)
                tokens_index(t, t % 2, at + 4)
                at += 4
                if t < 2:
                    slot_steps(t + 2, t % 2)
                if t == 0:
                    tile_experts()
                if t == 1:
                    tile_lo(0, 0)
            ve.wait_ge(s_b2, 16)

            def step(t, par, at, e, e_y):
                def tile(u):
                    return not isinstance(u, int) or 0 <= u < TILES

                other, tokens = 1 - par, tile(t + 3)
                gate(t, par, e)
                if tile(t - 2):
                    bias_y(t - 2, par, e_y)
                if tile(t + 4):
                    slot_steps(t + 4, par)
                split_hi(t, par, 0)
                if tokens:
                    tokens_compare(t + 3, other)
                split_lo(par, 0, at + 1)
                if tile(t + 1):
                    tile_lo(t + 1, other)
                n = 1
                if tokens:
                    tokens_count(other, at + 3)
                    n = 4
                split_hi(t, par, 1)
                if tokens:
                    tokens_place(other, at + 4)
                split_lo(par, 1, at + n + 1)
                if tokens:
                    tokens_index(t + 3, other, at + 6)
                return 6 if tokens else 2

            base = at
            es = experts(ve, 0)
            LT = step(0, 0, base, es[2], None)
            for t in range(1, 4):
                step(t, t % 2, t * LT + base, es[2 + t], es[t])
            with ve.Fori(4, TILES - 7, 4) as i:
                es = experts(ve, i)
                for q in range(4):
                    step(i + q, q % 2, (i + q) * LT + base, es[2 + q], es[q])
            at = (TILES - 7) * LT + base
            for t in range(TILES - 7, TILES):
                q = (t - TILES + 7) % 4
                if q == 0:
                    es = experts(ve, t)
                at += step(t, t % 2, at, es[2 + q], es[q])
            bias_y(TILES - 2, 1, es[3])
            bias_y(TILES - 1, 0, es[4])


def constants():
    import numpy as np

    c = np.zeros((P, C_END), np.float32)
    q = np.arange(P)
    c[:, C_ID:C_ID + P] = np.eye(P)
    c[:, C_SLOT:C_SLOT + P] = q
    t = np.arange(72)
    c[:, C_NEGT:C_NEGT + 72] = -P * t
    c[:, C_SLOTCOL:C_SLOTCOL + 72] = P * t + q[:, None]
    c[:, C_Q] = q
    pair = np.arange(NBLK)
    for i, v in enumerate((pair % NJ // JB, pair % JB)):
        step = np.diff(v, prepend=0)
        for h in range(NH):
            c[:, C_DJ + 2 * h + i] = step[h * P:(h + 1) * P]
    c[:, C_DESC:C_DESC + E] = E - np.arange(E)
    c[:, C_TOK2] = T
    c[:, C_TOK2 + 1] = 1
    c[:, C_T128:C_T128 + 72] = P * t
    c16 = np.ones((P, 2 * P), np.float16)
    c16[:, 0:P] = q[:, None] <= q
    return c, c16


_INS = ["x", "itok_B_6_14"] + ["L0_cond_" + n for n in (
    "ln_g", "ln_b", "subj_emb", "hyp_w1", "hyp_b1", "hyp_w2", "hyp_b2", "sty_w1", "sty_b1", "sty_w2", "sty_b2",
    "router_w", "exp_w1", "exp_b1", "exp_w2", "exp_b2")]


def kernel(**inputs):
    import numpy as np
    import concourse.bacc as bacc
    from concourse.bass_utils import run_bass_kernel_spmd

    nc = bacc.Bacc("TRN2", target_bir_lowering=False, num_devices=1)
    arrays, args = {}, []
    named = [(n, np.ascontiguousarray(inputs[n])) for n in _INS] + list(zip(("consts", "consts16"), constants()))
    for name, a in named:
        arrays[f"in_{name}"] = a
        args.append(nc.dram_tensor(f"in_{name}", a.shape, mybir.dt.from_np(a.dtype), kind="ExternalInput").ap())
    args.append(nc.dram_tensor("out_rows", (ROWS, D), F32, kind="ExternalOutput").ap())
    moe_kernel(nc, *args)
    r = run_bass_kernel_spmd(nc, [arrays], core_ids=[0])
    return r.results[0]["out_rows"][:N].reshape(B, T, D)
```
